# Optimizing a Trainium2 kernel written in Bass

```python
import numpy as np
import jax
import jax.numpy as jnp

def _softmax(x, axis=-1):
    return jax.nn.softmax(x, axis=axis)
def _gelu(x):
    return jax.nn.gelu(x, approximate=True)
def _silu(x):
    return jax.nn.silu(x)
def _sigmoid(x):
    return jax.nn.sigmoid(x)
def _layernorm(x, axis=-1, eps=1e-5):
    m = jnp.mean(x, axis=axis, keepdims=True)
    v = jnp.var(x, axis=axis, keepdims=True)
    return (x - m) / jnp.sqrt(v + eps)
def _scatter_add(tgt, idx, src, axis=0):
    return tgt.at[idx].add(src)
def _segment_sum(src, seg, n):
    return jax.ops.segment_sum(src, seg, n)

kernel_name = 'mk_adj_resnorm_d2_adj_256_8a5bd3'

def setup_inputs(seed: int = 0):
    np.random.seed(seed)
    _w = jnp.asarray
    def _rec_inputs():
        import jax
        import jax.numpy as jnp
        _gk = jax.random.key(seed)
        x = -0.0005207 + 1.001 * jax.random.normal(jax.random.fold_in(_gk, 1), (8, 2048, 256), jnp.float32)
        _a = jax.random.bernoulli(jax.random.fold_in(_gk, 2), 0.0078125, (2048, 2048))
        _a = jnp.logical_or(_a, jnp.swapaxes(_a, -1, -2))
        _a = jnp.logical_or(_a, jnp.eye(2048, dtype=bool))
        adj = _a.astype(jnp.int32)
        return x, adj
    x, adj = _rec_inputs()
    def _L0_gnn_setup():
        import jax, jax.numpy as jnp
        import numpy as np
        import math
        CHUNK = 256
        NUM_HEADS = 4
        EPS = 1e-05
        key = jax.random.key(seed)
        ks = jax.random.split(key, 12)
        B, N, F = (4, 2048, 256)
        x = jax.random.normal(ks[0], (B, N, F), dtype=jnp.float32)
        adj_matrix = jax.random.randint(ks[1], (N, N), 0, 2, dtype=jnp.int32)
        s = 1.0 / math.sqrt(F)
        Wq = jax.random.normal(ks[2], (F, F), dtype=jnp.float32) * s
        bq = jnp.zeros((F,), dtype=jnp.float32)
        Wk = jax.random.normal(ks[3], (F, F), dtype=jnp.float32) * s
        bk = jnp.zeros((F,), dtype=jnp.float32)
        Wv = jax.random.normal(ks[4], (F, F), dtype=jnp.float32) * s
        bv = jnp.zeros((F,), dtype=jnp.float32)
        Wo = jax.random.normal(ks[5], (F, F), dtype=jnp.float32) * s
        bo = jnp.zeros((F,), dtype=jnp.float32)
        gamma = jnp.ones((F,), dtype=jnp.float32)
        beta = jnp.zeros((F,), dtype=jnp.float32)
        return {'x': x, 'adj_matrix': adj_matrix, 'Wq': Wq, 'bq': bq, 'Wk': Wk, 'bk': bk, 'Wv': Wv, 'bv': bv, 'Wo': Wo, 'bo': bo, 'gamma': gamma, 'beta': beta}
    _L0_gnn_all = _L0_gnn_setup()
    _L0_gnn_in = {k: v for k, v in _L0_gnn_all.items() if k in ('Wq', 'bq', 'Wk', 'bk', 'Wv', 'bv', 'Wo', 'bo', 'gamma', 'beta', )}
    del _L0_gnn_all

    def _L1_gnn_setup():
        import jax, jax.numpy as jnp
        import numpy as np
        LEAKY_ALPHA = 0.2
        key = jax.random.key(seed)
        k1, k2, k3, k4 = jax.random.split(key, 4)
        B, N, Fin, Fout = (8, 2048, 256, 256)
        h = jax.random.normal(k1, (B, N, Fin), dtype=jnp.float32)
        adj = jax.random.randint(k2, (N, N), 0, 2, dtype=jnp.int32)
        W = jax.random.normal(k3, (Fin, Fout), dtype=jnp.float32) * (1.414 * (6.0 / (Fin + Fout)) ** 0.5)
        a = jax.random.normal(k4, (2 * Fout, 1), dtype=jnp.float32) * (1.414 * (6.0 / (2 * Fout + 1)) ** 0.5)
        return {'h': h, 'adj': adj, 'W': W, 'a': a}
    _L1_gnn_all = _L1_gnn_setup()
    _L1_gnn_in = {k: v for k, v in _L1_gnn_all.items() if k in ('W', 'a', )}
    del _L1_gnn_all

    return {
        "x": x,
        "adj": adj,
        "L0_gnn_Wq": _L0_gnn_in["Wq"],
        "L0_gnn_bq": _L0_gnn_in["bq"],
        "L0_gnn_Wk": _L0_gnn_in["Wk"],
        "L0_gnn_bk": _L0_gnn_in["bk"],
        "L0_gnn_Wv": _L0_gnn_in["Wv"],
        "L0_gnn_bv": _L0_gnn_in["bv"],
        "L0_gnn_Wo": _L0_gnn_in["Wo"],
        "L0_gnn_bo": _L0_gnn_in["bo"],
        "L0_gnn_gamma": _L0_gnn_in["gamma"],
        "L0_gnn_beta": _L0_gnn_in["beta"],
        "L1_gnn_W": _L1_gnn_in["W"],
        "L1_gnn_a": _L1_gnn_in["a"],
    }

def reference(x, adj, L0_gnn_Wq, L0_gnn_bq, L0_gnn_Wk, L0_gnn_bk, L0_gnn_Wv, L0_gnn_bv, L0_gnn_Wo, L0_gnn_bo, L0_gnn_gamma, L0_gnn_beta, L1_gnn_W, L1_gnn_a):
    import jax
    import jax.numpy as jnp
    def _L0_gnn_ref(x, adj_matrix, Wq, bq, Wk, bk, Wv, bv, Wo, bo, gamma, beta):
        import jax, jax.numpy as jnp
        import numpy as np
        import math
        CHUNK = 256
        NUM_HEADS = 4
        EPS = 1e-05
        B, N, Fin = x.shape
        H = NUM_HEADS
        Dout = Wq.shape[0]
        Dh = Dout // H
        Nc = N // CHUNK
        q = (x @ Wq.T + bq).reshape(B, N, H, Dh).transpose(0, 2, 1, 3)
        k = (x @ Wk.T + bk).reshape(B, N, H, Dh).transpose(0, 2, 1, 3)
        v = (x @ Wv.T + bv).reshape(B, N, H, Dh).transpose(0, 2, 1, 3)
        kc = k.reshape(B, H, Nc, CHUNK, Dh)
        vc = v.reshape(B, H, Nc, CHUNK, Dh)
        scores = jnp.einsum('bhnd,bhjcd->bhnjc', q, kc) / jnp.sqrt(jnp.asarray(Dh, dtype=q.dtype))
        scores = jnp.clip(scores, -10.0, 10.0)
        mask = adj_matrix.reshape(N, Nc, CHUNK)[None, None]
        scores = jnp.where(mask == 0, jnp.asarray(-10.0, scores.dtype), scores)
        attn = jax.nn.softmax(scores, axis=-1)
        ctx = jnp.einsum('bhnjc,bhjcd->bhnd', attn, vc)
        ctx = ctx.transpose(0, 2, 1, 3).reshape(B, N, Dout)
        out = ctx @ Wo.T + bo
        out = out + x
        mu = jnp.mean(out, axis=-1, keepdims=True)
        var = jnp.mean(jnp.square(out - mu), axis=-1, keepdims=True)
        out = (out - mu) * jax.lax.rsqrt(var + EPS) * gamma + beta
        return out

    def _L1_gnn_ref(h, adj, W, a):
        import jax, jax.numpy as jnp
        import numpy as np
        LEAKY_ALPHA = 0.2
        Fout = W.shape[1]
        Wh = jnp.einsum('bnf,fo->bno', h, W)
        a1 = a[:Fout, 0]
        a2 = a[Fout:, 0]
        s_i = Wh @ a1
        s_j = Wh @ a2
        e = jax.nn.leaky_relu(s_i[:, :, None] + s_j[:, None, :], negative_slope=LEAKY_ALPHA)
        N = Wh.shape[1]
        mask = (adj > 0) | jnp.eye(N, dtype=bool)
        e = jnp.where(mask[None, :, :], e, -jnp.inf)
        attention = jax.nn.softmax(e, axis=-1)
        attention = jnp.nan_to_num(attention, nan=0.0)
        h_prime = jnp.einsum('bij,bjo->bio', attention, Wh)
        return jax.nn.elu(h_prime)

    x = _layernorm(x + _L0_gnn_ref(x, adj, L0_gnn_Wq, L0_gnn_bq, L0_gnn_Wk, L0_gnn_bk, L0_gnn_Wv, L0_gnn_bv, L0_gnn_Wo, L0_gnn_bo, L0_gnn_gamma, L0_gnn_beta), axis=-1)
    x = _layernorm(x + _L1_gnn_ref(x, adj, L1_gnn_W, L1_gnn_a), axis=-1)
    return x


_drawn_inputs = setup_inputs


def setup_inputs(seed=0):
    import zlib

    import numpy as np

    out = dict(_drawn_inputs(seed))
    spreads = {'L0_gnn_bq': (0.0, 0.1),
     'L0_gnn_bk': (0.0, 2.0),
     'L0_gnn_bv': (0.0, 0.1),
     'L0_gnn_bo': (0.0, 0.1),
     'L0_gnn_gamma': (1.0, 0.2),
     'L0_gnn_beta': (0.0, 0.1)}
    factors = {}
    for name, (base, spread) in spreads.items():
        noise = np.random.default_rng([zlib.crc32(name.encode()), seed]).standard_normal(out[name].shape)
        drawn = base * np.exp(spread * noise) if base else spread * noise
        out[name] = jnp.asarray(drawn.astype(out[name].dtype))
    for name, factor in factors.items():
        out[name] = (out[name] * factor).astype(out[name].dtype)
    return out
```

```python
from contextlib import ExitStack

import concourse.bass as bass
from concourse import mybir

ALU = mybir.AluOpType
ACT = mybir.ActivationFunctionType
F32 = mybir.dt.float32
F32R = mybir.dt.float32r
BF16 = mybir.dt.bfloat16
I32 = mybir.dt.int32
I8 = mybir.dt.int8

P = 128
HEADS = 4
CLIP = 10.0
EPS = 1e-5
ALPHA = 0.2
BIG = 1.0e38

CW = 512
RING = 8
LAG = 4
SEG = 256


def layer0(nc, x, xT, adjT, wqT, wkT, wvT, woT, bq, bk, bv, bo, gamma, beta, x1):
    B, N, F = x.shape
    KB = F // P
    DH = F // HEADS
    PAIRS = HEADS // 2
    JB = N // P
    NC = N // CW
    T = CW // P
    ROUNDS = NC * PAIRS
    STEPS = ROUNDS * JB
    HALF = P // 2
    LIM = CLIP * DH ** 0.5
    KU = NC
    VU = JB // T
    USES = KU + VU + STEPS
    SJ = SEG // P
    SEGS = STEPS // SJ
    RSEGS = JB // SJ
    D_AT, I_AT, M_AT, A_AT = 5, 5, 7, 3
    assert SJ == 2
    PRJ = PAIRS * NC + T * NC

    q_use, wo_use, count = {}, {}, 0
    for p in range(PAIRS):
        q_use[0, p] = count
        count += 1
    for c in range(NC):
        if c + 1 < NC:
            q_use[c + 1, 0] = count
            count += 1
        if c >= 1:
            for t in range(T):
                wo_use[c - 1, t] = count
                count += 1
        if c + 1 < NC:
            q_use[c + 1, 1] = count
            count += 1
    for t in range(T):
        wo_use[NC - 1, t] = count
        count += 1
    assert count == PRJ

    with ExitStack() as ctx:
        def sb(name, shape, dt=F32):
            return ctx.enter_context(nc.sbuf_tensor(name, shape, dt))

        def sem(name):
            return ctx.enter_context(nc.semaphore(name))

        clip_hi = sb("clip_hi", [P, JB, N], I8)
        x_cols = sb("x_cols", [P, KB, N])
        k_split = sb("k_split", [P, HEADS, N], F32R)
        v_rows = sb("v_rows", [P, JB, F])
        q_hi = sb("q_hi", [P, 2, HEADS, CW], F32R)
        q_lo = sb("q_lo", [P, 2, HEADS, CW], F32R)
        probs = sb("probs", [P, RING, 2, CW])
        psums = sb("psums", [P, 2, 2, CW])
        inv_den = sb("inv_den", [P, 2, CW])
        seg_ctx = sb("seg_ctx", [P, 2, CW])
        ctx_t = sb("ctx_t", [P, 2, PAIRS, CW])
        x_rows = sb("x_rows", [P, 2, T, F])
        res = sb("res", [P, 2, T, F])
        wq = sb("wq", [P, KB, F])
        wk = sb("wk", [P, KB, F])
        wv = sb("wv", [P, KB, F])
        wo = sb("wo", [P, KB, F])
        bq_c = sb("bq_c", [P, PAIRS])
        bk_c = sb("bk_c", [P, PAIRS])
        bv_r = sb("bv_r", [P, F])
        bo_r = sb("bo_r", [P, F])
        gamma_r = sb("gamma_r", [P, F])
        beta_r = sb("beta_r", [P, F])
        ones = sb("ones", [P, HALF])
        bn = sb("bn", [P, 2, T, 6])
        mv = sb("mv", [P, 2, T, 2])
        var_eps = sb("var_eps", [P, 2, T])
        tick = sb("tick", [P, 1])
        minus_half = sb("minus_half", [P, T])
        rstd = sb("rstd", [P, 2, T])
        nmr = sb("nmr", [P, 2, T])

        sc_ps = ctx.enter_context(nc.psum_tensor("sc_ps", [P, 2, 2, CW], F32))
        ctx_ps = ctx.enter_context(nc.psum_tensor("ctx_ps", [P, 2, CW], F32))
        den_ps = ctx.enter_context(nc.psum_tensor("den_ps", [P, CW], F32))
        prj_ps = ctx.enter_context(nc.psum_tensor("prj_ps", [P, CW], F32))

        s_w = sem("weights_loaded")
        s_adj = [sem(f"adj_loaded{i}") for i in range(4)]
        s_flag = sem("adj_flagged")
        s_ones = sem("ones_set")
        s_xT = sem("x_cols_loaded")
        s_x = [sem("x_rows_loaded0"), sem("x_rows_loaded1")]
        s_xfree = sem("x_rows_used")
        s_fill = sem("slot_filled")
        s_read = sem("slot_read")
        s_khi = sem("k_hi_ready")
        s_klo = sem("k_lo_ready")
        s_v = sem("v_ready")
        s_prj = sem("prj_filled")
        s_prjfree = sem("prj_read")
        s_qhi = sem("q_hi_ready")
        s_qlo = sem("q_lo_ready")
        s_exp = sem("probs_ready")
        s_pv = sem("context_added")
        s_pool = sem("segment_summed")
        s_den = sem("den_ready")
        s_ln = sem("den_logged")
        s_inv = sem("den_inverted")
        s_norm = sem("segment_normed")
        s_acc = sem("segment_added")
        s_xb = sem("x_plus_bo")
        s_xbeta = sem("x_plus_beta")
        s_bn = [sem("stats_1"), sem("stats_2")]
        s_ag = [sem("mean_var_1"), sem("mean_var_2")]
        s_ve = [sem("var_eps_1"), sem("var_eps_2")]
        s_pw = [sem("rstd_1"), sem("rstd_2")]
        s_rs = [sem("nmr_1"), sem("nmr_2")]
        s_n = [sem("normed_1"), sem("normed_2")]
        s_gam = sem("times_gamma")
        s_z = sem("plus_x")
        s_x1 = [sem("x1_stored0"), sem("x1_stored1")]

        def head_rows(hh):
            return slice(HALF * hh, HALF * hh + HALF)

        stage = probs[:, :, :, :].rearrange("p (s a) h i -> p s (a h i)", s=4).bitcast(I32)
        adj_v = adjT.rearrange("(q a p) (c i) -> c q p a i", p=P, a=4, i=CW)

        block = ctx.enter_context(nc.Block())

        @block.sync
        def _(sp):
            for w, d in ((wk, wkT), (wv, wvT), (wq, wqT), (wo, woT)):
                sp.dma_start(w[:, :, :], d.rearrange("(k p) o -> p k o", p=P)).then_inc(s_w, 16)
            sp.dma_start(x_cols[:, :, :], xT[0].rearrange("(k p) n -> p k n", p=P)).then_inc(s_xT, 16)
            for i in range(NC * 4):
                if i >= 4:
                    sp.wait_ge(s_flag, 2 * (i - 3))
                sp.dma_start(stage[:, i % 4, :].rearrange("p (a i) -> p a i", a=4),
                             adj_v[i // 4, i % 4]).then_inc(s_adj[i % 4], 16)

            def load_rows(b, c):
                sp.wait_ge(s_xfree, b * NC + c + 1)
                sp.dma_start(x_rows[:, c % 2, :, :], x[b, c * CW:(c + 1) * CW, :]
                             .rearrange("(t p) f -> p t f", p=P)).then_inc(s_x[c % 2], 16)

            def store_x1(b, c):
                sp.wait_ge(s_n[1], (b * NC + c) * T + T)
                sp.dma_start(x1[b, c * CW:(c + 1) * CW, :].rearrange("(t p) f -> p t f", p=P),
                             res[:, c % 2, :, :]).then_inc(s_x1[c % 2], 16)

            def batch(b, last):
                load_rows(b, 0)
                load_rows(b, 1)
                load_rows(b, 2)
                store_x1(b, 0)
                load_rows(b, 3)
                if not last:
                    sp.wait_ge(s_prj, b * PRJ + q_use[NC - 1, 1] + 1)
                    sp.dma_start(x_cols[:, :, :], xT[b + 1].rearrange("(k p) n -> p k n", p=P))\
                      .then_inc(s_xT, 16)
                store_x1(b, 1)
                store_x1(b, 2)
                store_x1(b, 3)

            with sp.Fori(0, B - 1) as b:
                batch(b, False)
            batch(B - 1, True)
            for s in s_x1:
                sp.wait_ge(s, 16 + 16 * B * NC // 2)

        @block.gpsimd
        def _(pool):
            pool.memset(ones[:, :], 1.0).then_inc(s_ones, 1)
            pool.memset(minus_half[:, :], -0.5).then_inc(s_ones, 1)
            pool.wait_ge(s_ones, 2)
            pool.sem_inc(s_acc, 2)
            pool.sem_inc(s_pool, RING // SJ)

            def inverse_deviation(b, c, which):
                pool.wait_ge(s_ve[which], b * NC + c + 1)
                pool.tensor_tensor(rstd[:, which, :], var_eps[:, which, :], minus_half[:, :], ALU.pow)\
                    .then_inc(s_pw[which], 1)

            def add_segment(b, q):
                r, k = divmod(q, RSEGS)
                c, p = divmod(r, PAIRS)
                pool.wait_ge(s_norm, 2 + b * SEGS + q + 1)
                pool.wait_ge(s_acc, 2 + b * SEGS + q)
                if k == 0:
                    pool.sem_inc(s_acc, 1)
                    return
                pool.tensor_tensor(ctx_t[:, c % 2, p, :], ctx_t[:, c % 2, p, :], seg_ctx[:, q % 2, :],
                                   ALU.add).then_inc(s_acc, 1)

            with pool.Fori(0, B) as b:
                for q in range(SEGS):
                    r, k = divmod(q, RSEGS)
                    c, p = divmod(r, PAIRS)
                    pool.wait_ge(s_den, b * SEGS + q + 1)
                    pool.wait_ge(s_exp, b * STEPS + SJ * (q + 1))
                    pool.tensor_tensor(psums[:, q % 2, :, :], probs[:, (SJ * q) % RING, :, :],
                                       probs[:, (SJ * q + 1) % RING, :, :], ALU.add).then_inc(s_pool, 1)
                    if q >= A_AT:
                        add_segment(b, q - A_AT)
                    if k == 1 and p == 1 and c >= 1:
                        inverse_deviation(b, c - 1, 0)
                    if k == 1 and p == 0 and c >= 2:
                        inverse_deviation(b, c - 2, 1)
                inverse_deviation(b, NC - 2, 1)
                for q in range(SEGS - A_AT, SEGS):
                    add_segment(b, q)
                inverse_deviation(b, NC - 1, 0)
                inverse_deviation(b, NC - 1, 1)

        @block.scalar
        def _(act):
            for t, d in ((bv_r, bv), (bo_r, bo), (gamma_r, gamma), (beta_r, beta)):
                act.dma_start(t[:, :], d.partition_broadcast(P)).then_inc(s_w, 16)
            with nc.allow_non_contiguous_dma(reason="256 biases, once"):
                act.dma_start(bq_c[:, :], bq.rearrange("(k p) -> p k", p=P)).then_inc(s_w, 16)
                act.dma_start(bk_c[:, :], bk.rearrange("(k p) -> p k", p=P)).then_inc(s_w, 16)
            act.wait_ge(s_w, 160)

            def split_q_hi(b, c, p, k):
                hh, d = ((0, 0), (0, 1), (1, 1), (1, 0))[k]
                if k == 0:
                    act.wait_ge(s_prj, b * PRJ + q_use[c, p] + 1)
                r = head_rows(hh)
                act.activation(q_hi[head_rows(d), c % 2, 2 * p + hh, :], prj_ps[r, :], ACT.Identity,
                               bias=bq_c[r, p:p + 1]).then_inc(s_qhi, 1)

            def norm(b, c, t, which):
                if t == 0:
                    act.wait_ge(s_rs[which], b * NC + c + 1)
                    if which == 1:
                        act.wait_ge(s_z, 2 * (b * NC + c) + 2)
                act.activation(res[:, c % 2, t, :], res[:, c % 2, t, :], ACT.Identity,
                               scale=rstd[:, which, t:t + 1], bias=nmr[:, which, t:t + 1])\
                   .then_inc(s_n[which], 1)

            def invert(b, q):
                act.wait_ge(s_den, 2 + b * SEGS + q + 1)
                act.wait_ge(s_norm, b * SEGS + q + 1)
                act.activation(inv_den[:, q % 2, :], den_ps[:, :], ACT.Ln).then_inc(s_ln, 1)
                act.wait_ge(s_ln, 1 + b * SEGS + q + 1)
                act.activation(inv_den[:, q % 2, :], inv_den[:, q % 2, :], ACT.Exp, scale=-1.0)\
                   .then_inc(s_inv, 1)

            with act.Fori(0, B) as b:
                for c in range(NC):
                    u = c
                    act.wait_ge(s_fill, b * USES + u + 1)
                    for h in range(HEADS):
                        r = head_rows(h % 2)
                        act.activation(k_split[r, h, c * CW:(c + 1) * CW], sc_ps[r, u % 2, h // 2, :],
                                       ACT.Identity, bias=bk_c[r, h // 2:h // 2 + 1]).then_inc(s_khi, 1)
                for p in range(PAIRS):
                    for k in range(4):
                        split_q_hi(b, 0, p, k)
                for n in range(STEPS):
                    r, j = divmod(n, JB)
                    c, p = divmod(r, PAIRS)
                    act.wait_ge(s_read, 2 + b * USES + KU + VU + n + 1)
                    act.activation(probs[:, n % RING, :, :], probs[:, n % RING, :, :], ACT.Exp,
                                   scale=DH ** -0.5).then_inc(s_exp, 1)
                    if n >= I_AT and (n - I_AT) % SJ == 0:
                        invert(b, (n - I_AT) // SJ)
                    if c + 1 < NC and j <= 3:
                        split_q_hi(b, c + 1, p, j)
                    if c >= 1 and p == 1 and j in (4, 5, 7, 8):
                        norm(b, c - 1, (4, 5, 7, 8).index(j), 0)
                    if c >= 2 and p == 0 and j in (4, 5, 7, 8):
                        norm(b, c - 2, (4, 5, 7, 8).index(j), 1)
                for q in range((STEPS - I_AT + 1) // SJ, SEGS):
                    invert(b, q)
                for t in range(T):
                    norm(b, NC - 2, t, 1)
                for which in range(2):
                    for t in range(T):
                        norm(b, NC - 1, t, which)

        @block.tensor
        def _(pe):
            pe.sem_inc(s_pv, RING)
            pe.sem_inc(s_den, 2)
            pe.sem_inc(s_ln, 1)
            pe.wait_ge(s_w, 160)
            pe.wait_ge(s_ones, 1)

            def project_q(b, c, p):
                u = q_use[c, p]
                pe.wait_ge(s_prjfree, b * PRJ + u + 1)
                for k in range(KB):
                    last = pe.matmul(prj_ps[:, :], wq[:, k, p * P:(p + 1) * P],
                                     x_cols[:, k, c * CW:(c + 1) * CW], start=(k == 0), stop=(k == KB - 1))
                last.then_inc(s_prj, 1)

            def project_out(b, c, t):
                u = wo_use[c, t]
                pe.wait_ge(s_prjfree, b * PRJ + u + 1)
                if t == 0:
                    pe.wait_ge(s_acc, 2 + b * SEGS + PAIRS * RSEGS * (c + 1))
                for k in range(KB):
                    last = pe.matmul(prj_ps[:, 0:F], ctx_t[:, c % 2, k, t * P:(t + 1) * P], wo[:, k, :],
                                     start=(k == 0), stop=(k == KB - 1))
                last.then_inc(s_prj, 1)

            def scores(b, n):
                r, j = divmod(n, JB)
                c, p = divmod(r, PAIRS)
                u = KU + VU + n
                if j == 0:
                    pe.wait_ge(s_qlo, b * 8 * NC + 8 * c + 4 * (p + 1))
                    pe.wait_ge(s_qhi, b * 8 * NC + 8 * c + 4 * (p + 1))
                pe.wait_ge(s_read, b * USES + u + 1)
                for hh in range(2):
                    h = 2 * p + hh
                    lhs = k_split[:, h, j * P:(j + 1) * P]
                    pe.matmul(sc_ps[:, u % 2, hh, :], lhs, q_hi[:, c % 2, h, :], start=True, stop=False)
                    last = pe.matmul(sc_ps[:, u % 2, hh, :], lhs, q_lo[:, c % 2, h, :],
                                     start=False, stop=True)
                last.then_inc(s_fill, 1)

            def context(b, n):
                r, j = divmod(n, JB)
                p, q = r % PAIRS, n // SJ
                if n % SJ == 0:
                    pe.wait_ge(s_norm, b * SEGS + q + 1)
                pe.wait_ge(s_exp, b * STEPS + n + 1)
                for hh in range(2):
                    h = 2 * p + hh
                    last = pe.matmul(ctx_ps[head_rows(hh), q % 2, :], v_rows[:, j, h * DH:(h + 1) * DH],
                                     probs[:, n % RING, hh, :], start=(n % SJ == 0), stop=(n % SJ == SJ - 1))
                last.then_inc(s_pv, 1)

            def denominator(b, q):
                pe.wait_ge(s_pool, RING // SJ + b * SEGS + q + 1)
                pe.wait_ge(s_ln, b * SEGS + q + 1)
                for hh in range(2):
                    last = pe.matmul(den_ps[head_rows(hh), :], ones[:, :], psums[:, q % 2, hh, :],
                                     start=True, stop=True)
                last.then_inc(s_den, 1)

            with pe.Fori(0, B) as b:
                pe.wait_ge(s_xT, 16 * b + 16)
                for c in range(NC):
                    u = c
                    pe.wait_ge(s_read, b * USES + u + 1)
                    for p in range(PAIRS):
                        for k in range(KB):
                            last = pe.matmul(sc_ps[:, u % 2, p, :], wk[:, k, p * P:(p + 1) * P],
                                             x_cols[:, k, c * CW:(c + 1) * CW],
                                             start=(k == 0), stop=(k == KB - 1))
                    last.then_inc(s_fill, 1)
                for g in range(VU):
                    u = KU + g
                    pe.wait_ge(s_read, b * USES + u + 1)
                    v_ps = sc_ps[:, u % 2, :, :].rearrange("p h (t f) -> p (h t) f", f=F)
                    for t in range(T):
                        for k in range(KB):
                            last = pe.matmul(v_ps[:, t, :], x_cols[:, k, (g * T + t) * P:(g * T + t + 1) * P],
                                             wv[:, k, :], start=(k == 0), stop=(k == KB - 1))
                    last.then_inc(s_fill, 1)
                for p in range(PAIRS):
                    project_q(b, 0, p)
                pe.wait_ge(s_khi, 4 * NC * (b + 1))
                pe.wait_ge(s_klo, 4 * NC * (b + 1))
                pe.wait_ge(s_v, VU * (b + 1))
                for n in range(STEPS):
                    r, j = divmod(n, JB)
                    c, p = divmod(r, PAIRS)
                    scores(b, n)
                    if n >= LAG:
                        context(b, n - LAG)
                    if c + 1 < NC and j == 0:
                        project_q(b, c + 1, p)
                    if n >= D_AT and (n - D_AT) % SJ == 0:
                        denominator(b, (n - D_AT) // SJ)
                    if c >= 1 and p == 0 and 11 <= j <= 14:
                        project_out(b, c - 1, j - 11)
                for n in range(STEPS - LAG, STEPS):
                    context(b, n)
                for q in range((STEPS - D_AT + 1) // SJ, SEGS):
                    denominator(b, q)
                for t in range(T):
                    project_out(b, NC - 1, t)

        @block.vector
        def _(dve):
            dve.sem_inc(s_read, 2)
            dve.sem_inc(s_prjfree, 1)
            dve.sem_inc(s_norm, 2)
            dve.sem_inc(s_xfree, 2)
            for s in s_x1:
                dve.sem_inc(s, 16)
            for i in range(NC * 4):
                c, q = divmod(i, 4)
                dve.wait_ge(s_adj[i % 4], 16 * (i // 4 + 1))
                piece = stage[:, i % 4, :]
                dve.tensor_scalar(piece, piece, 0, int(2 * LIM), ALU.not_equal, ALU.mult).then_inc(s_flag, 1)
                dve.wait_ge(s_flag, 2 * i + 1)
                dve.tensor_scalar(clip_hi[:, 4 * q:4 * q + 4, c * CW:(c + 1) * CW],
                                  piece.rearrange("p (a i) -> p a i", a=4), -LIM, None, ALU.add)\
                   .then_inc(s_flag, 1)
            dve.wait_ge(s_flag, 2 * NC * 4)
            dve.wait_ge(s_w, 160)

            def split_q_lo(b, c, p, k):
                hh, d = ((0, 0), (0, 1), (1, 1), (1, 0))[k]
                r = head_rows(hh)
                if k == 0:
                    dve.wait_ge(s_qhi, b * 8 * NC + 8 * c + 4 * (p + 1))
                dve.scalar_tensor_tensor(out=q_lo[head_rows(d), c % 2, 2 * p + hh, :], in0=prj_ps[r, :],
                                         scalar=bq_c[r, p:p + 1],
                                         in1=q_hi[r, c % 2, 2 * p + hh, :].bitcast(F32),
                                         op0=ALU.add, op1=ALU.subtract).then_inc(s_qlo, 1)
                if k == 3:
                    dve.wait_ge(s_qlo, b * 8 * NC + 8 * c + 4 * (p + 1))
                    dve.sem_inc(s_prjfree, 1)

            def normalise(b, q):
                r, k = divmod(q, RSEGS)
                c, p = divmod(r, PAIRS)
                dve.wait_ge(s_inv, b * SEGS + q + 1)
                dve.wait_ge(s_pv, RING + b * STEPS + SJ * (q + 1))
                if k == 0:
                    to = ctx_t[:, c % 2, p, :]
                else:
                    dve.wait_ge(s_acc, b * SEGS + q + 1)
                    to = seg_ctx[:, q % 2, :]
                dve.tensor_tensor(to, ctx_ps[:, q % 2, :], inv_den[:, q % 2, :], ALU.mult).then_inc(s_norm, 1)

            def add_bo(b, c, half):
                g = b * NC + c
                two = slice(2 * half, 2 * half + 2)
                if half == 0:
                    dve.wait_ge(s_x[c % 2], 16 * (b * (NC // 2) + c // 2 + 1))
                    dve.wait_ge(s_x1[c % 2], 16 * (b * (NC // 2) + c // 2 + 1))
                dve.tensor_tensor(res[:, c % 2, two, :], x_rows[:, c % 2, two, :],
                                  bo_r[:, None, :].broadcast_to([P, 2, F]), ALU.add).then_inc(s_xb, 1)

            def add_beta(b, c, half):
                g = b * NC + c
                two = slice(2 * half, 2 * half + 2)
                dve.wait_ge(s_xb, 2 * g + 2)
                dve.tensor_tensor(x_rows[:, c % 2, two, :], x_rows[:, c % 2, two, :],
                                  beta_r[:, None, :].broadcast_to([P, 2, F]), ALU.add).then_inc(s_xbeta, 1)

            def add_projection(b, c, t):
                u = b * PRJ + wo_use[c, t]
                dve.wait_ge(s_prj, u + 1)
                dve.wait_ge(s_xb, 2 * (b * NC + c) + 2)
                dve.tensor_tensor(res[:, c % 2, t, :], prj_ps[:, 0:F], res[:, c % 2, t, :], ALU.add)\
                   .then_inc(s_prjfree, 1)

            def stats(b, c, t, which):
                g = b * NC + c
                if which == 0:
                    dve.wait_ge(s_prjfree, 1 + b * PRJ + wo_use[c, t] + 1)
                else:
                    dve.wait_ge(s_z, 2 * g + 1 + t // 2)
                dve.bn_stats(bn[:, which, t, :], res[:, c % 2, t, :]).then_inc(s_bn[which], 1)

            def aggregate(b, c, which):
                dve.wait_ge(s_bn[which], T * (b * NC + c + 1))
                dve.memset(tick[:, :], 0.0)
                for t in range(T):
                    dve.bn_aggr(mv[:, which, t, :], bn[:, which, t, :]).then_inc(s_ag[which], 1)

            def variance(b, c, which):
                g = b * NC + c
                aggregate(b, c, which)
                dve.wait_ge(s_ag[which], T * g + T)
                dve.tensor_scalar(var_eps[:, which, :], mv[:, which, :, 1], EPS, None, ALU.add)\
                   .then_inc(s_ve[which], 1)

            def offset(b, c, which):
                dve.wait_ge(s_pw[which], b * NC + c + 1)
                dve.scalar_tensor_tensor(out=nmr[:, which, :], in0=mv[:, which, :, 0], scalar=-1.0,
                                         in1=rstd[:, which, :], op0=ALU.mult, op1=ALU.mult)\
                   .then_inc(s_rs[which], 1)

            def times_gamma(b, c, half):
                g = b * NC + c
                two = slice(2 * half, 2 * half + 2)
                dve.wait_ge(s_n[0], T * g + 2 * (half + 1))
                dve.tensor_tensor(res[:, c % 2, two, :], res[:, c % 2, two, :],
                                  gamma_r[:, None, :].broadcast_to([P, 2, F]), ALU.mult).then_inc(s_gam, 1)

            def add_x(b, c, half):
                g = b * NC + c
                two = slice(2 * half, 2 * half + 2)
                dve.wait_ge(s_gam, 2 * g + 1 + half)
                dve.wait_ge(s_xbeta, 2 * g + 1 + half)
                dve.tensor_tensor(res[:, c % 2, two, :], res[:, c % 2, two, :],
                                  x_rows[:, c % 2, two, :], ALU.add).then_inc(s_z, 1)
                if half == 1:
                    dve.wait_ge(s_z, 2 * g + 2)
                    dve.sem_inc(s_xfree, 1)

            with dve.Fori(0, B) as b:
                for c in range(NC):
                    u = c
                    for h in range(HEADS):
                        r, o = head_rows(h % 2), head_rows(1 - h % 2)
                        dve.wait_ge(s_khi, b * 4 * NC + 4 * c + h + 1)
                        dve.scalar_tensor_tensor(
                            out=k_split[o, h, c * CW:(c + 1) * CW], in0=sc_ps[r, u % 2, h // 2, :],
                            scalar=bk_c[r, h // 2:h // 2 + 1],
                            in1=k_split[r, h, c * CW:(c + 1) * CW].bitcast(F32),
                            op0=ALU.add, op1=ALU.subtract).then_inc(s_klo, 1)
                    dve.wait_ge(s_klo, b * 4 * NC + 4 * c + 4)
                    dve.sem_inc(s_read, 1)
                for g in range(VU):
                    u = KU + g
                    dve.wait_ge(s_fill, b * USES + u + 1)
                    dve.tensor_tensor(v_rows[:, T * g:T * g + T, :],
                                      sc_ps[:, u % 2, :, :].rearrange("p h (t f) -> p (h t) f", f=F),
                                      bv_r[:, None, :].broadcast_to([P, T, F]), ALU.add).then_inc(s_v, 1)
                    dve.wait_ge(s_v, b * VU + g + 1)
                    dve.sem_inc(s_read, 1)
                for p in range(PAIRS):
                    for k in range(4):
                        split_q_lo(b, 0, p, k)
                for n in range(STEPS):
                    r, j = divmod(n, JB)
                    c, p = divmod(r, PAIRS)
                    u = KU + VU + n
                    dve.wait_ge(s_fill, b * USES + u + 1)
                    dve.wait_ge(s_pv, b * STEPS + n + 1)
                    if n % SJ == 0:
                        dve.wait_ge(s_pool, b * SEGS + n // SJ + 1)
                    dve.scalar_tensor_tensor(
                        out=probs[:, n % RING, :, :], in0=sc_ps[:, u % 2, :, :], scalar=-LIM,
                        in1=clip_hi[:, j, c * CW:(c + 1) * CW][:, None, :].broadcast_to([P, 2, CW]),
                        op0=ALU.max, op1=ALU.min).then_inc(s_read, 1)
                    if n >= M_AT and (n - M_AT) % SJ == 0:
                        normalise(b, (n - M_AT) // SJ)
                    if c + 1 < NC and j in (4, 5):
                        split_q_lo(b, c + 1, p, 2 * (j - 4))
                        split_q_lo(b, c + 1, p, 2 * (j - 4) + 1)
                    if c >= 1 and p == 0:
                        if j in (0, 1):
                            add_bo(b, c - 1, j)
                        if j == 3 and c >= 2:
                            offset(b, c - 2, 1)
                        if 12 <= j <= 15:
                            add_projection(b, c - 1, j - 12)
                            stats(b, c - 1, j - 12, 0)
                        if j == 15:
                            variance(b, c - 1, 0)
                    if c >= 1 and p == 1:
                        if j in (0, 1):
                            add_beta(b, c - 1, j)
                        if j == 3:
                            offset(b, c - 1, 0)
                        if j in (12, 13):
                            times_gamma(b, c - 1, j - 12)
                        if j in (13, 14):
                            add_x(b, c - 1, j - 13)
                        if j == 15:
                            for t in range(T):
                                stats(b, c - 1, t, 1)
                            variance(b, c - 1, 1)
                c = NC - 1
                add_bo(b, c, 0)
                add_bo(b, c, 1)
                offset(b, c - 1, 1)
                add_beta(b, c, 0)
                add_beta(b, c, 1)
                for q in range((STEPS - M_AT + 1) // SJ, SEGS):
                    normalise(b, q)
                for t in range(T):
                    add_projection(b, c, t)
                    stats(b, c, t, 0)
                variance(b, c, 0)
                offset(b, c, 0)
                for half in range(2):
                    times_gamma(b, c, half)
                for half in range(2):
                    add_x(b, c, half)
                for t in range(T):
                    stats(b, c, t, 1)
                variance(b, c, 1)
                offset(b, c, 1)


def layer1(nc, x1, adjT, W, a, out):
    B, N, F = x1.shape
    KB = F // P
    JB = N // P
    NC = N // CW
    T = CW // P
    STEPS = NC * JB
    ERING = 8
    AHEAD = 2
    OUT_BANKS = 6
    TU, SU, WU = KB * NC, NC, JB
    USES = TU + SU + WU

    with ExitStack() as ctx:
        def sb(name, shape, dt=F32):
            return ctx.enter_context(nc.sbuf_tensor(name, shape, dt))

        def sem(name):
            return ctx.enter_context(nc.semaphore(name))

        mask = sb("mask", [P, JB, N], BF16)
        x_in = sb("x_in", [P, JB, F])
        x_cols = sb("x1_cols", [P, KB, N])
        wh = sb("wh", [P, JB, F + 2])
        s_fifth = sb("s_fifth", [P, JB])
        s_row = sb("s_row", [P, N])
        best = sb("best", [P, N])
        low = sb("low", [P, N])
        e = sb("e", [P, ERING, CW])
        w_ext = sb("w_ext", [P, KB, F + 1])
        wa1 = sb("wa1", [P, KB])
        wa1_b = sb("wa1_b", [P, KB, P])
        a1_r = sb("a1_r", [P, F])
        a2_r = sb("a2_r", [P, F])
        trash = sb("trash", [P, 2 * KB, F])
        ident = sb("ident", [P, P])
        rden = sb("rden", [P, 2, T])
        h = sb("h", [P, 2, T, F])
        neg = sb("neg", [P, T, F])
        bn = sb("bn1", [P, T, 6])
        mv = sb("mv1", [P, T, 2])
        var_eps = sb("var_eps1", [P, T])
        tick = sb("tick1", [P, 1])
        pool_tick = sb("pool_tick", [P, 1])
        minus_half = sb("minus_half1", [P, T])
        rstd = sb("rstd1", [P, T])
        nmr = sb("nmr1", [P, T])
        stage = e[:, :, :].rearrange("p (s a) i -> p s (a i)", s=2).bitcast(I32)

        prep_ps = ctx.enter_context(nc.psum_tensor("prep_ps", [P, 2, CW], F32))
        out_ps = ctx.enter_context(nc.psum_tensor("out_ps", [P, OUT_BANKS, CW], F32))

        s_w = sem("b_weights_loaded")
        s_adj = [sem(f"b_adj_loaded{i}") for i in range(2)]
        s_mask = sem("mask_made")
        s_diag = sem("diagonal_set")
        s_id = sem("identity_made")
        s_wa = sem("wa_made")
        s_x = sem("x1_loaded")
        s_prep = sem("prep_filled")
        s_prepread = sem("prep_read")
        s_fifths = sem("s_fifth_made")
        s_best = sem("best_updated")
        s_all = sem("best_reduced")
        s_rows = sem("rows_made")
        s_lin = sem("low_side_ready")
        s_max = sem("larger_side_taken")
        s_log = sem("logits_masked")
        s_e = sem("exp_ready")
        s_mm = sem("products_added")
        s_out = sem("chunk_summed")
        s_rd = sem("denominators_inverted")
        s_h = sem("h_scaled")
        s_min = sem("h_below_zero")
        s_en = sem("h_exp")
        s_elu = sem("elu_made")
        s_r = sem("residual_added")
        s_bn = sem("b_stats")
        s_ag = sem("b_mean_var")
        s_ve = sem("b_var_eps")
        s_pw = sem("b_rstd")
        s_rs = sem("b_nmr")
        s_y = sem("out_normed")
        s_st = [sem("out_stored0"), sem("out_stored1")]

        adj_v = adjT.rearrange("(q a p) (c i) -> c q p a i", p=P, a=4, i=CW)

        block = ctx.enter_context(nc.Block())

        @block.sync
        def _(sp):
            sp.dma_start(w_ext[:, :, 1:F + 1], W.rearrange("(k p) o -> p k o", p=P)).then_inc(s_w, 16)
            for r, i in ((a1_r, 0), (a2_r, 1)):
                sp.dma_start(r[:, :], a.rearrange("(s o) one -> s (o one)", s=2)[i].partition_broadcast(P))\
                  .then_inc(s_w, 16)
            for i in range(NC * 4):
                if i >= 2:
                    sp.wait_ge(s_mask, i - 1)
                sp.dma_start(stage[:, i % 2, :].rearrange("p (a i) -> p a i", a=4),
                             adj_v[i // 4, i % 4]).then_inc(s_adj[i % 2], 16)
            with sp.Fori(0, B) as b:
                sp.wait_ge(s_r, NC * b + NC)
                sp.dma_start(x_in[:, :, :], x1[b].rearrange("(j p) f -> p j f", p=P)).then_inc(s_x, 16)
                for c in range(NC):
                    sp.wait_ge(s_y, T * (b * NC + c + 1))
                    sp.dma_start(out[b, c * CW:(c + 1) * CW, :].rearrange("(t p) f -> p t f", p=P),
                                 h[:, c % 2, :, :]).then_inc(s_st[c % 2], 16)
            for s in s_st:
                sp.wait_ge(s, 16 + 16 * B * NC // 2)

        @block.gpsimd
        def _(pool):
            pool.memset(ident[:, :], 0.0).then_inc(s_id, 1)
            pool.memset(wh[:, :, F + 1:F + 2], 1.0).then_inc(s_id, 1)
            pool.memset(minus_half[:, :], -0.5).then_inc(s_id, 1)
            pool.wait_ge(s_id, 3)
            pool.affine_select(out=ident[:, :], in_=ident[:, :], compare_op=ALU.not_equal, fill=1.0,
                               base=0, pattern=[[-1, P]], channel_multiplier=1).then_inc(s_id, 1)
            pool.wait_ge(s_mask, NC * 4)
            for j in range(JB):
                diag = mask[:, j, j * P:(j + 1) * P]
                pool.affine_select(out=diag, in_=diag, compare_op=ALU.not_equal, fill=0.0,
                                   base=0, pattern=[[-1, P]], channel_multiplier=1).then_inc(s_diag, 1)
            with pool.Fori(0, B) as b:
                pool.wait_ge(s_best, JB * (b + 1))
                pool.wait_ge(s_max, STEPS * b + 1)
                pool.tensor_tensor(pool_tick[:, :], minus_half[:, 0:1], minus_half[:, 1:2], ALU.add)
                pool.partition_all_reduce(low[:, :], best[:, :], P, bass.bass_isa.ReduceOp.max)\
                    .then_inc(s_all, 1)
                for c in range(NC):
                    pool.wait_ge(s_ve, b * NC + c + 1)
                    pool.tensor_tensor(rstd[:, :], var_eps[:, :], minus_half[:, :], ALU.pow).then_inc(s_pw, 1)

        def scale_h(act, b, c):
            g = b * NC + c
            act.wait_ge(s_rd, T * (g + 1))
            act.wait_ge(s_st[c % 2], 16 * (b * (NC // 2) + c // 2 + 1))
            for t in range(T):
                act.activation(h[:, c % 2, t, :], out_ps[:, (T * c + t) % OUT_BANKS, 0:F], ACT.Identity,
                               scale=rden[:, c % 2, t:t + 1]).then_inc(s_h, 1)

        def exp_h(act, b, c):
            act.wait_ge(s_min, b * NC + c + 1)
            act.activation(neg[:, :, :], neg[:, :, :], ACT.Exp).then_inc(s_en, 1)

        def norm_h(act, b, c):
            act.wait_ge(s_rs, b * NC + c + 1)
            for t in range(T):
                act.activation(h[:, c % 2, t, :], h[:, c % 2, t, :], ACT.Identity,
                               scale=rstd[:, t:t + 1], bias=nmr[:, t:t + 1]).then_inc(s_y, 1)

        @block.scalar
        def _(act):
            act.sem_inc(s_prepread, 2)
            act.wait_ge(s_w, 48)
            with act.Fori(0, B) as b:
                for u in range(USES):
                    act.wait_ge(s_prep, b * USES + u + 1)
                    if u < TU:
                        dst = x_cols[:, u // NC, (u % NC) * CW:(u % NC + 1) * CW]
                        src = prep_ps[:, u % 2, :]
                    elif u < TU + SU:
                        c = u - TU
                        dst = s_row[:, c * CW:(c + 1) * CW]
                        src = prep_ps[:, u % 2, :]
                    else:
                        dst = wh[:, u - TU - SU, 0:F + 1]
                        src = prep_ps[:, u % 2, 0:F + 1]
                    act.activation(dst, src, ACT.Copy).then_inc(s_prepread, 1)

                def low_side(n):
                    c, j = divmod(n, JB)
                    act.wait_ge(s_mm, b * STEPS + n + 1)
                    act.activation(e[:, n % ERING, :], low[:, c * CW:(c + 1) * CW], ACT.Identity,
                                   bias=s_fifth[:, j:j + 1]).then_inc(s_lin, 1)

                act.wait_ge(s_rows, 4 * (b + 1))
                act.wait_ge(s_fifths, b + 1)
                for n in range(AHEAD):
                    low_side(n)
                for n in range(STEPS):
                    c, j = divmod(n, JB)
                    if n + AHEAD < STEPS:
                        low_side(n + AHEAD)
                    act.wait_ge(s_log, b * STEPS + n + 1)
                    act.activation(e[:, n % ERING, :], e[:, n % ERING, :], ACT.Exp).then_inc(s_e, 1)
                    if c >= 1 and j == 3:
                        scale_h(act, b, c - 1)
                    if c >= 1 and j == 8:
                        exp_h(act, b, c - 1)
                    if c >= 2 and j == 0:
                        norm_h(act, b, c - 2)
                norm_h(act, b, NC - 2)
                scale_h(act, b, NC - 1)
                exp_h(act, b, NC - 1)
                norm_h(act, b, NC - 1)

        @block.tensor
        def _(pe):
            pe.sem_inc(s_mm, ERING)
            pe.wait_ge(s_id, 4)
            pe.wait_ge(s_wa, 2 * KB + KB)
            with pe.Fori(0, B) as b:
                pe.wait_ge(s_x, 16 * (b + 1))
                for u in range(USES):
                    pe.wait_ge(s_prepread, b * USES + u + 1)
                    if u < TU:
                        k, g = divmod(u, NC)
                        for t in range(T):
                            last = pe.transpose(prep_ps[:, u % 2, t * P:(t + 1) * P],
                                                x_in[:, g * T + t, k * P:(k + 1) * P], ident[:, :])
                    elif u < TU + SU:
                        if u == TU:
                            pe.wait_ge(s_prepread, 2 + b * USES + TU)
                        c = u - TU
                        for k in range(KB):
                            last = pe.matmul(prep_ps[:, u % 2, :], wa1_b[:, k, :],
                                             x_cols[:, k, c * CW:(c + 1) * CW],
                                             start=(k == 0), stop=(k == KB - 1))
                    else:
                        j = u - TU - SU
                        for k in range(KB):
                            last = pe.matmul(prep_ps[:, u % 2, 0:F + 1], x_cols[:, k, j * P:(j + 1) * P],
                                             w_ext[:, k, :], start=(k == 0), stop=(k == KB - 1))
                    last.then_inc(s_prep, 1)
                pe.wait_ge(s_prepread, 2 + (b + 1) * USES)
                for n in range(STEPS):
                    c, j = divmod(n, JB)
                    pe.wait_ge(s_e, b * STEPS + n + 1)
                    for t in range(T):
                        if j == 0:
                            pe.wait_ge(s_h, b * NC * T + c * T + t + 1)
                        last = pe.matmul(out_ps[:, (T * c + t) % OUT_BANKS, 0:F + 1],
                                         e[:, n % ERING, t * P:(t + 1) * P], wh[:, j, 1:F + 2],
                                         start=(j == 0), stop=(j == JB - 1))
                    last.then_inc(s_mm, 1)

        @block.vector
        def _(dve):
            dve.sem_inc(s_r, NC)
            dve.sem_inc(s_max, 1)
            dve.sem_inc(s_h, OUT_BANKS)
            for s in s_st:
                dve.sem_inc(s, 16)
            dve.wait_ge(s_w, 48)
            for k in range(KB):
                for i, (row, dst) in enumerate(((a1_r, wa1[:, k:k + 1]), (a2_r, w_ext[:, k, 0:1]))):
                    dve.tensor_tensor_reduce(out=trash[:, 2 * k + i, :], in0=w_ext[:, k, 1:F + 1], in1=row[:, :],
                                             scale=1.0, scalar=0.0, op0=ALU.mult, op1=ALU.add,
                                             accum_out=dst).then_inc(s_wa, 1)
            dve.wait_ge(s_wa, 2 * KB)
            dve.wait_ge(s_id, 1)
            for k in range(KB):
                dve.tensor_scalar(wa1_b[:, k, :], a1_r[:, 0:P], 0.0, wa1[:, k:k + 1], ALU.mult, ALU.add)\
                   .then_inc(s_wa, 1)
            for i in range(NC * 4):
                c, q = divmod(i, 4)
                dve.wait_ge(s_adj[i % 2], 16 * (i // 2 + 1))
                dve.tensor_scalar(mask[:, 4 * q:4 * q + 4, c * CW:(c + 1) * CW],
                                  stage[:, i % 2, :].rearrange("p (a i) -> p a i", a=4),
                                  0, -BIG, ALU.is_le, ALU.mult).then_inc(s_mask, 1)
            dve.wait_ge(s_diag, JB)

            def invert(b, c):
                g = b * NC + c
                dve.wait_ge(s_mm, ERING + b * STEPS + (c + 1) * JB)
                for t in range(T):
                    dve.reciprocal(rden[:, c % 2, t:t + 1],
                                   out_ps[:, (T * c + t) % OUT_BANKS, F:F + 1]).then_inc(s_rd, 1)

            def below_zero(b, c):
                g = b * NC + c
                dve.wait_ge(s_h, OUT_BANKS + T * (g + 1))
                dve.tensor_scalar(neg[:, :, :], h[:, c % 2, :, :], 0.0, None, ALU.min).then_inc(s_min, 1)

            def elu(b, c):
                g = b * NC + c
                dve.wait_ge(s_en, g + 1)
                dve.scalar_tensor_tensor(out=h[:, c % 2, :, :], in0=h[:, c % 2, :, :], scalar=0.0,
                                         in1=neg[:, :, :], op0=ALU.max, op1=ALU.add).then_inc(s_elu, 1)

            def residual(b, c):
                g = b * NC + c
                dve.wait_ge(s_elu, g + 1)
                dve.scalar_tensor_tensor(out=h[:, c % 2, :, :], in0=h[:, c % 2, :, :], scalar=-1.0,
                                         in1=x_in[:, T * c:T * c + T, :], op0=ALU.add, op1=ALU.add)\
                   .then_inc(s_r, 1)

            def stats(b, c, t):
                g = b * NC + c
                dve.wait_ge(s_r, NC + g + 1)
                dve.bn_stats(bn[:, t, :], h[:, c % 2, t, :]).then_inc(s_bn, 1)

            def aggregate(b, c):
                dve.wait_ge(s_bn, T * (b * NC + c + 1))
                dve.memset(tick[:, :], 0.0)
                for t in range(T):
                    dve.bn_aggr(mv[:, t, :], bn[:, t, :]).then_inc(s_ag, 1)

            def variance(b, c):
                aggregate(b, c)
                dve.wait_ge(s_ag, T * (b * NC + c + 1))
                dve.wait_ge(s_y, T * (b * NC + c))
                dve.tensor_scalar(var_eps[:, :], mv[:, :, 1], EPS, None, ALU.add).then_inc(s_ve, 1)

            def offset(b, c):
                dve.wait_ge(s_pw, b * NC + c + 1)
                dve.scalar_tensor_tensor(out=nmr[:, :], in0=mv[:, :, 0], scalar=-1.0, in1=rstd[:, :],
                                         op0=ALU.mult, op1=ALU.mult).then_inc(s_rs, 1)

            with dve.Fori(0, B) as b:
                dve.wait_ge(s_prepread, 2 + (b + 1) * USES)
                dve.tensor_scalar(s_fifth[:, :], wh[:, :, 0], ALPHA, None, ALU.mult).then_inc(s_fifths, 1)
                for j in range(JB):
                    if j == 0:
                        dve.tensor_scalar(best[:, :], mask[:, 0, :], wh[:, 0, 0:1], None, ALU.add)\
                           .then_inc(s_best, 1)
                    else:
                        dve.wait_ge(s_best, b * JB + j)
                        dve.scalar_tensor_tensor(out=best[:, :], in0=mask[:, j, :], scalar=wh[:, j, 0:1],
                                                 in1=best[:, :], op0=ALU.add, op1=ALU.max).then_inc(s_best, 1)
                dve.wait_ge(s_all, b + 1)
                dve.tensor_tensor(low[:, :], low[:, :], s_row[:, :], ALU.add).then_inc(s_rows, 1)
                dve.wait_ge(s_rows, 4 * b + 1)
                dve.scalar_tensor_tensor(out=low[:, :], in0=low[:, :], scalar=ALPHA, in1=low[:, :],
                                         op0=ALU.mult, op1=ALU.max).then_inc(s_rows, 1)
                dve.wait_ge(s_rows, 4 * b + 2)
                dve.tensor_tensor(best[:, :], s_row[:, :], low[:, :], ALU.subtract).then_inc(s_rows, 1)
                dve.scalar_tensor_tensor(out=low[:, :], in0=s_row[:, :], scalar=ALPHA, in1=low[:, :],
                                         op0=ALU.mult, op1=ALU.subtract).then_inc(s_rows, 1)
                dve.wait_ge(s_rows, 4 * b + 4)
                for n in range(STEPS):
                    c, j = divmod(n, JB)
                    tile = e[:, n % ERING, :]
                    dve.wait_ge(s_lin, b * STEPS + n + 1)
                    dve.scalar_tensor_tensor(out=tile, in0=best[:, c * CW:(c + 1) * CW], scalar=wh[:, j, 0:1],
                                             in1=tile, op0=ALU.add, op1=ALU.max).then_inc(s_max, 1)
                    dve.wait_ge(s_max, 1 + b * STEPS + n + 1)
                    dve.tensor_tensor(tile, tile, mask[:, j, c * CW:(c + 1) * CW], ALU.add).then_inc(s_log, 1)
                    if c >= 1:
                        if j == 2:
                            invert(b, c - 1)
                        if j == 6:
                            below_zero(b, c - 1)
                        if j == 10:
                            elu(b, c - 1)
                        if j == 11:
                            residual(b, c - 1)
                        if j == 12:
                            for t in range(T):
                                stats(b, c - 1, t)
                        if j == 13:
                            variance(b, c - 1)
                        if j == 15:
                            offset(b, c - 1)
                c = NC - 1
                invert(b, c)
                below_zero(b, c)
                elu(b, c)
                residual(b, c)
                for t in range(T):
                    stats(b, c, t)
                variance(b, c)
                offset(b, c)


def build(nc, x, xT, adjT, wqT, wkT, wvT, woT, bq, bk, bv, bo, gamma, beta, W, a, out):
    x1 = nc.dram_tensor("x1", tuple(x.shape), F32, kind="Internal").ap()
    layer0(nc, x, xT, adjT, wqT, wkT, wvT, woT, bq, bk, bv, bo, gamma, beta, x1)
    layer1(nc, x1, adjT, W, a, out)


def kernel(x, adj, L0_gnn_Wq, L0_gnn_bq, L0_gnn_Wk, L0_gnn_bk, L0_gnn_Wv, L0_gnn_bv, L0_gnn_Wo, L0_gnn_bo,
           L0_gnn_gamma, L0_gnn_beta, L1_gnn_W, L1_gnn_a):
    import numpy as np
    import concourse.bacc as bacc
    from concourse.bass_utils import run_bass_kernel_spmd

    x = np.asarray(x)
    arrays = {
        "x": x, "xT": x.transpose(0, 2, 1), "adjT": np.asarray(adj).T,
        "wqT": np.asarray(L0_gnn_Wq).T, "wkT": np.asarray(L0_gnn_Wk).T,
        "wvT": np.asarray(L0_gnn_Wv).T, "woT": np.asarray(L0_gnn_Wo).T,
        "bq": np.asarray(L0_gnn_bq), "bk": np.asarray(L0_gnn_bk), "bv": np.asarray(L0_gnn_bv),
        "bo": np.asarray(L0_gnn_bo), "gamma": np.asarray(L0_gnn_gamma), "beta": np.asarray(L0_gnn_beta),
        "W": np.asarray(L1_gnn_W), "a": np.asarray(L1_gnn_a),
    }
    arrays = {name: np.ascontiguousarray(v) for name, v in arrays.items()}
    nc = bacc.Bacc("TRN2", target_bir_lowering=False, num_devices=1, dynamic_dma_scratch_size=8192)
    args = [nc.dram_tensor(f"in_{name}", v.shape, mybir.dt.from_np(v.dtype), kind="ExternalInput").ap()
            for name, v in arrays.items()]
    out = nc.dram_tensor("out_0", x.shape, F32, kind="ExternalOutput").ap()
    build(nc, *args, out)
    r = run_bass_kernel_spmd(nc, [{f"in_{name}": v for name, v in arrays.items()}], core_ids=[0])
    return r.results[0]["out_0"]
```

```python
from contextlib import ExitStack

import concourse.bass as bass
from concourse import mybir

ALU = mybir.AluOpType
ACT = mybir.ActivationFunctionType
F32 = mybir.dt.float32
F32R = mybir.dt.float32r
BF16 = mybir.dt.bfloat16
I32 = mybir.dt.int32
I8 = mybir.dt.int8

P = 128
HEADS = 4
CLIP = 10.0
EPS = 1e-5
ALPHA = 0.2
BIG = 1.0e38

CW = 512
RING = 8
LAG = 4
SEG = 256


def layer0(nc, x, xT, adjT, wqT, wkT, wvT, woT, bq, bk, bv, bo, gamma, beta, x1):
    B, N, F = x.shape
    KB = F // P
    DH = F // HEADS
    PAIRS = HEADS // 2
    JB = N // P
    NC = N // CW
    T = CW // P
    ROUNDS = NC * PAIRS
    STEPS = ROUNDS * JB
    HALF = P // 2
    LIM = CLIP * DH ** 0.5
    KU = NC
    VU = JB // T
    USES = KU + VU + STEPS
    SJ = SEG // P
    SEGS = STEPS // SJ
    RSEGS = JB // SJ
    D_AT, I_AT, M_AT, A_AT = 5, 5, 7, 3
    assert SJ == 2
    PRJ = PAIRS * NC + T * NC

    q_use, wo_use, count = {}, {}, 0
    for p in range(PAIRS):
        q_use[0, p] = count
        count += 1
    for c in range(NC):
        if c + 1 < NC:
            q_use[c + 1, 0] = count
            count += 1
        if c >= 1:
            for t in range(T):
                wo_use[c - 1, t] = count
                count += 1
        if c + 1 < NC:
            q_use[c + 1, 1] = count
            count += 1
    for t in range(T):
        wo_use[NC - 1, t] = count
        count += 1
    assert count == PRJ

    with ExitStack() as ctx:
        def sb(name, shape, dt=F32):
            return ctx.enter_context(nc.sbuf_tensor(name, shape, dt))

        def sem(name):
            return ctx.enter_context(nc.semaphore(name))

        clip_hi = sb("clip_hi", [P, JB, N], I8)
        x_cols = sb("x_cols", [P, KB, N])
        k_split = sb("k_split", [P, HEADS, N], F32R)
        v_rows = sb("v_rows", [P, JB, F])
        q_hi = sb("q_hi", [P, 2, HEADS, CW], F32R)
        q_lo = sb("q_lo", [P, 2, HEADS, CW], F32R)
        probs = sb("probs", [P, RING, 2, CW])
        psums = sb("psums", [P, 2, 2, CW])
        inv_den = sb("inv_den", [P, 2, CW])
        seg_ctx = sb("seg_ctx", [P, 2, CW])
        ctx_t = sb("ctx_t", [P, 2, PAIRS, CW])
        x_rows = sb("x_rows", [P, 2, T, F])
        res = sb("res", [P, 2, T, F])
        wq = sb("wq", [P, KB, F])
        wk = sb("wk", [P, KB, F])
        wv = sb("wv", [P, KB, F])
        wo = sb("wo", [P, KB, F])
        bq_c = sb("bq_c", [P, PAIRS])
        bk_c = sb("bk_c", [P, PAIRS])
        bv_r = sb("bv_r", [P, F])
        bo_r = sb("bo_r", [P, F])
        gamma_r = sb("gamma_r", [P, F])
        beta_r = sb("beta_r", [P, F])
        ones = sb("ones", [P, HALF])
        bn = sb("bn", [P, 2, T, 6])
        mv = sb("mv", [P, 2, T, 2])
        var_eps = sb("var_eps", [P, 2, T])
        tick = sb("tick", [P, 1])
        minus_half = sb("minus_half", [P, T])
        rstd = sb("rstd", [P, 2, T])
        nmr = sb("nmr", [P, 2, T])

        sc_ps = ctx.enter_context(nc.psum_tensor("sc_ps", [P, 2, 2, CW], F32))
        ctx_ps = ctx.enter_context(nc.psum_tensor("ctx_ps", [P, 2, CW], F32))
        den_ps = ctx.enter_context(nc.psum_tensor("den_ps", [P, CW], F32))
        prj_ps = ctx.enter_context(nc.psum_tensor("prj_ps", [P, CW], F32))

        s_w = sem("weights_loaded")
        s_adj = [sem(f"adj_loaded{i}") for i in range(4)]
        s_flag = sem("adj_flagged")
        s_ones = sem("ones_set")
        s_xT = sem("x_cols_loaded")
        s_x = [sem("x_rows_loaded0"), sem("x_rows_loaded1")]
        s_xfree = sem("x_rows_used")
        s_fill = sem("slot_filled")
        s_read = sem("slot_read")
        s_khi = sem("k_hi_ready")
        s_klo = sem("k_lo_ready")
        s_v = sem("v_ready")
        s_prj = sem("prj_filled")
        s_prjfree = sem("prj_read")
        s_qhi = sem("q_hi_ready")
        s_qlo = sem("q_lo_ready")
        s_exp = sem("probs_ready")
        s_pv = sem("context_added")
        s_pool = sem("segment_summed")
        s_den = sem("den_ready")
        s_ln = sem("den_logged")
        s_inv = sem("den_inverted")
        s_norm = sem("segment_normed")
        s_acc = sem("segment_added")
        s_xb = sem("x_plus_bo")
        s_xbeta = sem("x_plus_beta")
        s_bn = [sem("stats_1"), sem("stats_2")]
        s_ag = [sem("mean_var_1"), sem("mean_var_2")]
        s_ve = [sem("var_eps_1"), sem("var_eps_2")]
        s_pw = [sem("rstd_1"), sem("rstd_2")]
        s_rs = [sem("nmr_1"), sem("nmr_2")]
        s_n = [sem("normed_1"), sem("normed_2")]
        s_gam = sem("times_gamma")
        s_z = sem("plus_x")
        s_x1 = [sem("x1_stored0"), sem("x1_stored1")]

        def head_rows(hh):
            return slice(HALF * hh, HALF * hh + HALF)

        stage = probs[:, :, :, :].rearrange("p (s a) h i -> p s (a h i)", s=4).bitcast(I32)
        adj_v = adjT.rearrange("(q a p) (c i) -> c q p a i", p=P, a=4, i=CW)

        block = ctx.enter_context(nc.Block())

        @block.sync
        def _(sp):
            for w, d in ((wk, wkT), (wv, wvT), (wq, wqT), (wo, woT)):
                sp.dma_start(w[:, :, :], d.rearrange("(k p) o -> p k o", p=P)).then_inc(s_w, 16)
            sp.dma_start(x_cols[:, :, :], xT[0].rearrange("(k p) n -> p k n", p=P)).then_inc(s_xT, 16)
            for i in range(NC * 4):
                if i >= 4:
                    sp.wait_ge(s_flag, 2 * (i - 3))
                sp.dma_start(stage[:, i % 4, :].rearrange("p (a i) -> p a i", a=4),
                             adj_v[i // 4, i % 4]).then_inc(s_adj[i % 4], 16)

            def load_rows(b, c):
                sp.wait_ge(s_xfree, b * NC + c + 1)
                sp.dma_start(x_rows[:, c % 2, :, :], x[b, c * CW:(c + 1) * CW, :]
                             .rearrange("(t p) f -> p t f", p=P)).then_inc(s_x[c % 2], 16)

            def store_x1(b, c):
                sp.wait_ge(s_n[1], (b * NC + c) * T + T)
                sp.dma_start(x1[b, c * CW:(c + 1) * CW, :].rearrange("(t p) f -> p t f", p=P),
                             res[:, c % 2, :, :]).then_inc(s_x1[c % 2], 16)

            def batch(b, last):
                load_rows(b, 0)
                load_rows(b, 1)
                load_rows(b, 2)
                store_x1(b, 0)
                load_rows(b, 3)
                if not last:
                    sp.wait_ge(s_prj, b * PRJ + q_use[NC - 1, 1] + 1)
                    sp.dma_start(x_cols[:, :, :], xT[b + 1].rearrange("(k p) n -> p k n", p=P))\
                      .then_inc(s_xT, 16)
                store_x1(b, 1)
                store_x1(b, 2)
                store_x1(b, 3)

            with sp.Fori(0, B - 1) as b:
                batch(b, False)
            batch(B - 1, True)
            for s in s_x1:
                sp.wait_ge(s, 16 + 16 * B * NC // 2)

        @block.gpsimd
        def _(pool):
            pool.memset(ones[:, :], 1.0).then_inc(s_ones, 1)
            pool.memset(minus_half[:, :], -0.5).then_inc(s_ones, 1)
            pool.wait_ge(s_ones, 2)
            pool.sem_inc(s_acc, 2)
            pool.sem_inc(s_pool, RING // SJ)

            def inverse_deviation(b, c, which):
                pool.wait_ge(s_ve[which], b * NC + c + 1)
                pool.tensor_tensor(rstd[:, which, :], var_eps[:, which, :], minus_half[:, :], ALU.pow)\
                    .then_inc(s_pw[which], 1)

            def add_segment(b, q):
                r, k = divmod(q, RSEGS)
                c, p = divmod(r, PAIRS)
                pool.wait_ge(s_norm, 2 + b * SEGS + q + 1)
                pool.wait_ge(s_acc, 2 + b * SEGS + q)
                if k == 0:
                    pool.sem_inc(s_acc, 1)
                    return
                pool.tensor_tensor(ctx_t[:, c % 2, p, :], ctx_t[:, c % 2, p, :], seg_ctx[:, q % 2, :],
                                   ALU.add).then_inc(s_acc, 1)

            with pool.Fori(0, B) as b:
                for q in range(SEGS):
                    r, k = divmod(q, RSEGS)
                    c, p = divmod(r, PAIRS)
                    pool.wait_ge(s_den, b * SEGS + q + 1)
                    pool.wait_ge(s_exp, b * STEPS + SJ * (q + 1))
                    pool.tensor_tensor(psums[:, q % 2, :, :], probs[:, (SJ * q) % RING, :, :],
                                       probs[:, (SJ * q + 1) % RING, :, :], ALU.add).then_inc(s_pool, 1)
                    if q >= A_AT:
                        add_segment(b, q - A_AT)
                    if k == 1 and p == 1 and c >= 1:
                        inverse_deviation(b, c - 1, 0)
                    if k == 1 and p == 0 and c >= 2:
                        inverse_deviation(b, c - 2, 1)
                inverse_deviation(b, NC - 2, 1)
                for q in range(SEGS - A_AT, SEGS):
                    add_segment(b, q)
                inverse_deviation(b, NC - 1, 0)
                inverse_deviation(b, NC - 1, 1)

        @block.scalar
        def _(act):
            for t, d in ((bv_r, bv), (bo_r, bo), (gamma_r, gamma), (beta_r, beta)):
                act.dma_start(t[:, :], d.partition_broadcast(P)).then_inc(s_w, 16)
            with nc.allow_non_contiguous_dma(reason="256 biases, once"):
                act.dma_start(bq_c[:, :], bq.rearrange("(k p) -> p k", p=P)).then_inc(s_w, 16)
                act.dma_start(bk_c[:, :], bk.rearrange("(k p) -> p k", p=P)).then_inc(s_w, 16)
            act.preload_act_table_set("natural_log_exp_and_others")
            act.wait_ge(s_w, 160)

            def split_q_hi(b, c, p, k):
                hh, d = ((0, 0), (0, 1), (1, 1), (1, 0))[k]
                if k == 0:
                    act.wait_ge(s_prj, b * PRJ + q_use[c, p] + 1)
                r = head_rows(hh)
                act.activation(q_hi[head_rows(d), c % 2, 2 * p + hh, :], prj_ps[r, :], ACT.Identity,
                               bias=bq_c[r, p:p + 1]).then_inc(s_qhi, 1)

            def norm(b, c, t, which):
                if t == 0:
                    act.wait_ge(s_rs[which], b * NC + c + 1)
                    if which == 1:
                        act.wait_ge(s_z, 2 * (b * NC + c) + 2)
                act.activation(res[:, c % 2, t, :], res[:, c % 2, t, :], ACT.Identity,
                               scale=rstd[:, which, t:t + 1], bias=nmr[:, which, t:t + 1])\
                   .then_inc(s_n[which], 1)

            def invert(b, q):
                act.wait_ge(s_den, 2 + b * SEGS + q + 1)
                act.wait_ge(s_norm, b * SEGS + q + 1)
                act.activation(inv_den[:, q % 2, :], den_ps[:, :], ACT.Ln).then_inc(s_ln, 1)
                act.wait_ge(s_ln, 1 + b * SEGS + q + 1)
                act.activation(inv_den[:, q % 2, :], inv_den[:, q % 2, :], ACT.Exp, scale=-1.0)\
                   .then_inc(s_inv, 1)

            with act.Fori(0, B) as b:
                for c in range(NC):
                    u = c
                    act.wait_ge(s_fill, b * USES + u + 1)
                    for h in range(HEADS):
                        r = head_rows(h % 2)
                        act.activation(k_split[r, h, c * CW:(c + 1) * CW], sc_ps[r, u % 2, h // 2, :],
                                       ACT.Identity, bias=bk_c[r, h // 2:h // 2 + 1]).then_inc(s_khi, 1)
                for p in range(PAIRS):
                    for k in range(4):
                        split_q_hi(b, 0, p, k)
                for n in range(STEPS):
                    r, j = divmod(n, JB)
                    c, p = divmod(r, PAIRS)
                    act.wait_ge(s_read, 2 + b * USES + KU + VU + n + 1)
                    act.activation(probs[:, n % RING, :, :], probs[:, n % RING, :, :], ACT.Exp,
                                   scale=DH ** -0.5).then_inc(s_exp, 1)
                    if n >= I_AT and (n - I_AT) % SJ == 0:
                        invert(b, (n - I_AT) // SJ)
                    if c + 1 < NC and j <= 3:
                        split_q_hi(b, c + 1, p, j)
                    if c >= 1 and p == 1 and j in (4, 5, 7, 8):
                        norm(b, c - 1, (4, 5, 7, 8).index(j), 0)
                    if c >= 2 and p == 0 and j in (4, 5, 7, 8):
                        norm(b, c - 2, (4, 5, 7, 8).index(j), 1)
                for q in range((STEPS - I_AT + 1) // SJ, SEGS):
                    invert(b, q)
                for t in range(T):
                    norm(b, NC - 2, t, 1)
                for which in range(2):
                    for t in range(T):
                        norm(b, NC - 1, t, which)

        @block.tensor
        def _(pe):
            pe.sem_inc(s_pv, RING)
            pe.sem_inc(s_den, 2)
            pe.sem_inc(s_ln, 1)
            pe.wait_ge(s_w, 160)
            pe.wait_ge(s_ones, 1)

            def project_q(b, c, p):
                u = q_use[c, p]
                pe.wait_ge(s_prjfree, b * PRJ + u + 1)
                for k in range(KB):
                    last = pe.matmul(prj_ps[:, :], wq[:, k, p * P:(p + 1) * P],
                                     x_cols[:, k, c * CW:(c + 1) * CW], start=(k == 0), stop=(k == KB - 1))
                last.then_inc(s_prj, 1)

            def project_out(b, c, t):
                u = wo_use[c, t]
                pe.wait_ge(s_prjfree, b * PRJ + u + 1)
                if t == 0:
                    pe.wait_ge(s_acc, 2 + b * SEGS + PAIRS * RSEGS * (c + 1))
                for k in range(KB):
                    last = pe.matmul(prj_ps[:, 0:F], ctx_t[:, c % 2, k, t * P:(t + 1) * P], wo[:, k, :],
                                     start=(k == 0), stop=(k == KB - 1))
                last.then_inc(s_prj, 1)

            def scores(b, n):
                r, j = divmod(n, JB)
                c, p = divmod(r, PAIRS)
                u = KU + VU + n
                if j == 0:
                    pe.wait_ge(s_qlo, b * 8 * NC + 8 * c + 4 * (p + 1))
                    pe.wait_ge(s_qhi, b * 8 * NC + 8 * c + 4 * (p + 1))
                pe.wait_ge(s_read, b * USES + u + 1)
                for hh in range(2):
                    h = 2 * p + hh
                    lhs = k_split[:, h, j * P:(j + 1) * P]
                    pe.matmul(sc_ps[:, u % 2, hh, :], lhs, q_hi[:, c % 2, h, :], start=True, stop=False)
                    last = pe.matmul(sc_ps[:, u % 2, hh, :], lhs, q_lo[:, c % 2, h, :],
                                     start=False, stop=True)
                last.then_inc(s_fill, 1)

            def context(b, n):
                r, j = divmod(n, JB)
                p, q = r % PAIRS, n // SJ
                if n % SJ == 0:
                    pe.wait_ge(s_norm, b * SEGS + q + 1)
                pe.wait_ge(s_exp, b * STEPS + n + 1)
                for hh in range(2):
                    h = 2 * p + hh
                    last = pe.matmul(ctx_ps[head_rows(hh), q % 2, :], v_rows[:, j, h * DH:(h + 1) * DH],
                                     probs[:, n % RING, hh, :], start=(n % SJ == 0), stop=(n % SJ == SJ - 1))
                last.then_inc(s_pv, 1)

            def denominator(b, q):
                pe.wait_ge(s_pool, RING // SJ + b * SEGS + q + 1)
                pe.wait_ge(s_ln, b * SEGS + q + 1)
                for hh in range(2):
                    last = pe.matmul(den_ps[head_rows(hh), :], ones[:, :], psums[:, q % 2, hh, :],
                                     start=True, stop=True)
                last.then_inc(s_den, 1)

            with pe.Fori(0, B) as b:
                pe.wait_ge(s_xT, 16 * b + 16)
                for c in range(NC):
                    u = c
                    pe.wait_ge(s_read, b * USES + u + 1)
                    for p in range(PAIRS):
                        for k in range(KB):
                            last = pe.matmul(sc_ps[:, u % 2, p, :], wk[:, k, p * P:(p + 1) * P],
                                             x_cols[:, k, c * CW:(c + 1) * CW],
                                             start=(k == 0), stop=(k == KB - 1))
                    last.then_inc(s_fill, 1)
                for g in range(VU):
                    u = KU + g
                    pe.wait_ge(s_read, b * USES + u + 1)
                    v_ps = sc_ps[:, u % 2, :, :].rearrange("p h (t f) -> p (h t) f", f=F)
                    for t in range(T):
                        for k in range(KB):
                            last = pe.matmul(v_ps[:, t, :], x_cols[:, k, (g * T + t) * P:(g * T + t + 1) * P],
                                             wv[:, k, :], start=(k == 0), stop=(k == KB - 1))
                    last.then_inc(s_fill, 1)
                for p in range(PAIRS):
                    project_q(b, 0, p)
                pe.wait_ge(s_khi, 4 * NC * (b + 1))
                pe.wait_ge(s_klo, 4 * NC * (b + 1))
                pe.wait_ge(s_v, VU * (b + 1))
                for n in range(STEPS):
                    r, j = divmod(n, JB)
                    c, p = divmod(r, PAIRS)
                    scores(b, n)
                    if n >= LAG:
                        context(b, n - LAG)
                    if c + 1 < NC and j == 0:
                        project_q(b, c + 1, p)
                    if n >= D_AT and (n - D_AT) % SJ == 0:
                        denominator(b, (n - D_AT) // SJ)
                    if c >= 1 and p == 0 and 11 <= j <= 14:
                        project_out(b, c - 1, j - 11)
                for n in range(STEPS - LAG, STEPS):
                    context(b, n)
                for q in range((STEPS - D_AT + 1) // SJ, SEGS):
                    denominator(b, q)
                for t in range(T):
                    project_out(b, NC - 1, t)

        @block.vector
        def _(dve):
            dve.sem_inc(s_read, 2)
            dve.sem_inc(s_prjfree, 1)
            dve.sem_inc(s_norm, 2)
            dve.sem_inc(s_xfree, 2)
            for s in s_x1:
                dve.sem_inc(s, 16)
            for i in range(NC * 4):
                c, q = divmod(i, 4)
                dve.wait_ge(s_adj[i % 4], 16 * (i // 4 + 1))
                piece = stage[:, i % 4, :]
                dve.tensor_scalar(piece, piece, 0, int(2 * LIM), ALU.not_equal, ALU.mult).then_inc(s_flag, 1)
                dve.wait_ge(s_flag, 2 * i + 1)
                dve.tensor_scalar(clip_hi[:, 4 * q:4 * q + 4, c * CW:(c + 1) * CW],
                                  piece.rearrange("p (a i) -> p a i", a=4), -LIM, None, ALU.add)\
                   .then_inc(s_flag, 1)
            dve.wait_ge(s_flag, 2 * NC * 4)
            dve.wait_ge(s_w, 160)

            def split_q_lo(b, c, p, k):
                hh, d = ((0, 0), (0, 1), (1, 1), (1, 0))[k]
                r = head_rows(hh)
                if k == 0:
                    dve.wait_ge(s_qhi, b * 8 * NC + 8 * c + 4 * (p + 1))
                dve.scalar_tensor_tensor(out=q_lo[head_rows(d), c % 2, 2 * p + hh, :], in0=prj_ps[r, :],
                                         scalar=bq_c[r, p:p + 1],
                                         in1=q_hi[r, c % 2, 2 * p + hh, :].bitcast(F32),
                                         op0=ALU.add, op1=ALU.subtract).then_inc(s_qlo, 1)
                if k == 3:
                    dve.wait_ge(s_qlo, b * 8 * NC + 8 * c + 4 * (p + 1))
                    dve.sem_inc(s_prjfree, 1)

            def normalise(b, q):
                r, k = divmod(q, RSEGS)
                c, p = divmod(r, PAIRS)
                dve.wait_ge(s_inv, b * SEGS + q + 1)
                dve.wait_ge(s_pv, RING + b * STEPS + SJ * (q + 1))
                if k == 0:
                    to = ctx_t[:, c % 2, p, :]
                else:
                    dve.wait_ge(s_acc, b * SEGS + q + 1)
                    to = seg_ctx[:, q % 2, :]
                dve.tensor_tensor(to, ctx_ps[:, q % 2, :], inv_den[:, q % 2, :], ALU.mult).then_inc(s_norm, 1)

            def add_bo(b, c, half):
                g = b * NC + c
                two = slice(2 * half, 2 * half + 2)
                if half == 0:
                    dve.wait_ge(s_x[c % 2], 16 * (b * (NC // 2) + c // 2 + 1))
                    dve.wait_ge(s_x1[c % 2], 16 * (b * (NC // 2) + c // 2 + 1))
                dve.tensor_tensor(res[:, c % 2, two, :], x_rows[:, c % 2, two, :],
                                  bo_r[:, None, :].broadcast_to([P, 2, F]), ALU.add).then_inc(s_xb, 1)

            def add_beta(b, c, half):
                g = b * NC + c
                two = slice(2 * half, 2 * half + 2)
                dve.wait_ge(s_xb, 2 * g + 2)
                dve.tensor_tensor(x_rows[:, c % 2, two, :], x_rows[:, c % 2, two, :],
                                  beta_r[:, None, :].broadcast_to([P, 2, F]), ALU.add).then_inc(s_xbeta, 1)

            def add_projection(b, c, t):
                u = b * PRJ + wo_use[c, t]
                dve.wait_ge(s_prj, u + 1)
                dve.wait_ge(s_xb, 2 * (b * NC + c) + 2)
                dve.tensor_tensor(res[:, c % 2, t, :], prj_ps[:, 0:F], res[:, c % 2, t, :], ALU.add)\
                   .then_inc(s_prjfree, 1)

            def stats(b, c, t, which):
                g = b * NC + c
                if which == 0:
                    dve.wait_ge(s_prjfree, 1 + b * PRJ + wo_use[c, t] + 1)
                else:
                    dve.wait_ge(s_z, 2 * g + 1 + t // 2)
                dve.bn_stats(bn[:, which, t, :], res[:, c % 2, t, :]).then_inc(s_bn[which], 1)

            def aggregate(b, c, which):
                dve.wait_ge(s_bn[which], T * (b * NC + c + 1))
                dve.memset(tick[:, :], 0.0)
                for t in range(T):
                    dve.bn_aggr(mv[:, which, t, :], bn[:, which, t, :]).then_inc(s_ag[which], 1)

            def variance(b, c, which):
                g = b * NC + c
                aggregate(b, c, which)
                dve.wait_ge(s_ag[which], T * g + T)
                dve.tensor_scalar(var_eps[:, which, :], mv[:, which, :, 1], EPS, None, ALU.add)\
                   .then_inc(s_ve[which], 1)

            def offset(b, c, which):
                dve.wait_ge(s_pw[which], b * NC + c + 1)
                dve.scalar_tensor_tensor(out=nmr[:, which, :], in0=mv[:, which, :, 0], scalar=-1.0,
                                         in1=rstd[:, which, :], op0=ALU.mult, op1=ALU.mult)\
                   .then_inc(s_rs[which], 1)

            def times_gamma(b, c, half):
                g = b * NC + c
                two = slice(2 * half, 2 * half + 2)
                dve.wait_ge(s_n[0], T * g + 2 * (half + 1))
                dve.tensor_tensor(res[:, c % 2, two, :], res[:, c % 2, two, :],
                                  gamma_r[:, None, :].broadcast_to([P, 2, F]), ALU.mult).then_inc(s_gam, 1)

            def add_x(b, c, half):
                g = b * NC + c
                two = slice(2 * half, 2 * half + 2)
                dve.wait_ge(s_gam, 2 * g + 1 + half)
                dve.wait_ge(s_xbeta, 2 * g + 1 + half)
                dve.tensor_tensor(res[:, c % 2, two, :], res[:, c % 2, two, :],
                                  x_rows[:, c % 2, two, :], ALU.add).then_inc(s_z, 1)
                if half == 1:
                    dve.wait_ge(s_z, 2 * g + 2)
                    dve.sem_inc(s_xfree, 1)

            with dve.Fori(0, B) as b:
                for c in range(NC):
                    u = c
                    for h in range(HEADS):
                        r, o = head_rows(h % 2), head_rows(1 - h % 2)
                        dve.wait_ge(s_khi, b * 4 * NC + 4 * c + h + 1)
                        dve.scalar_tensor_tensor(
                            out=k_split[o, h, c * CW:(c + 1) * CW], in0=sc_ps[r, u % 2, h // 2, :],
                            scalar=bk_c[r, h // 2:h // 2 + 1],
                            in1=k_split[r, h, c * CW:(c + 1) * CW].bitcast(F32),
                            op0=ALU.add, op1=ALU.subtract).then_inc(s_klo, 1)
                    dve.wait_ge(s_klo, b * 4 * NC + 4 * c + 4)
                    dve.sem_inc(s_read, 1)
                for g in range(VU):
                    u = KU + g
                    dve.wait_ge(s_fill, b * USES + u + 1)
                    dve.tensor_tensor(v_rows[:, T * g:T * g + T, :],
                                      sc_ps[:, u % 2, :, :].rearrange("p h (t f) -> p (h t) f", f=F),
                                      bv_r[:, None, :].broadcast_to([P, T, F]), ALU.add).then_inc(s_v, 1)
                    dve.wait_ge(s_v, b * VU + g + 1)
                    dve.sem_inc(s_read, 1)
                for p in range(PAIRS):
                    for k in range(4):
                        split_q_lo(b, 0, p, k)
                for n in range(STEPS):
                    r, j = divmod(n, JB)
                    c, p = divmod(r, PAIRS)
                    u = KU + VU + n
                    dve.wait_ge(s_fill, b * USES + u + 1)
                    dve.wait_ge(s_pv, b * STEPS + n + 1)
                    if n % SJ == 0:
                        dve.wait_ge(s_pool, b * SEGS + n // SJ + 1)
                    dve.scalar_tensor_tensor(
                        out=probs[:, n % RING, :, :], in0=sc_ps[:, u % 2, :, :], scalar=-LIM,
                        in1=clip_hi[:, j, c * CW:(c + 1) * CW][:, None, :].broadcast_to([P, 2, CW]),
                        op0=ALU.max, op1=ALU.min).then_inc(s_read, 1)
                    if n >= M_AT and (n - M_AT) % SJ == 0:
                        normalise(b, (n - M_AT) // SJ)
                    if c + 1 < NC and j in (4, 5):
                        split_q_lo(b, c + 1, p, 2 * (j - 4))
                        split_q_lo(b, c + 1, p, 2 * (j - 4) + 1)
                    if c >= 1 and p == 0:
                        if j in (0, 1):
                            add_bo(b, c - 1, j)
                        if j == 3 and c >= 2:
                            offset(b, c - 2, 1)
                        if 12 <= j <= 15:
                            add_projection(b, c - 1, j - 12)
                            stats(b, c - 1, j - 12, 0)
                        if j == 15:
                            variance(b, c - 1, 0)
                    if c >= 1 and p == 1:
                        if j in (0, 1):
                            add_beta(b, c - 1, j)
                        if j == 3:
                            offset(b, c - 1, 0)
                        if j in (12, 13):
                            times_gamma(b, c - 1, j - 12)
                        if j in (13, 14):
                            add_x(b, c - 1, j - 13)
                        if j == 15:
                            for t in range(T):
                                stats(b, c - 1, t, 1)
                            variance(b, c - 1, 1)
                c = NC - 1
                add_bo(b, c, 0)
                add_bo(b, c, 1)
                offset(b, c - 1, 1)
                add_beta(b, c, 0)
                add_beta(b, c, 1)
                for q in range((STEPS - M_AT + 1) // SJ, SEGS):
                    normalise(b, q)
                for t in range(T):
                    add_projection(b, c, t)
                    stats(b, c, t, 0)
                variance(b, c, 0)
                offset(b, c, 0)
                for half in range(2):
                    times_gamma(b, c, half)
                for half in range(2):
                    add_x(b, c, half)
                for t in range(T):
                    stats(b, c, t, 1)
                variance(b, c, 1)
                offset(b, c, 1)


def layer1(nc, x1, adjT, W, a, out):
    B, N, F = x1.shape
    KB = F // P
    JB = N // P
    NC = N // CW
    T = CW // P
    STEPS = NC * JB
    ERING = 8
    AHEAD = 2
    OUT_BANKS = 6
    TU, SU, WU = KB * NC, NC, JB
    USES = TU + SU + WU
    PE_AT, ACT_AT = 2, 6
    assert NC * T == JB and B % 2 == 0 and B >= 4 and ACT_AT + USES <= STEPS - AHEAD

    def max_at(j):
        return 22 + j * 29 // JB

    ROWS_AT = 58

    def count(b, per, n=0):
        i, s = b
        return i * (2 * per) + (s * per + n)

    def of_batch(d, b):
        i, s = b
        return d.rearrange("(i s) n f -> i s n f", s=2)[i + s // 2, s % 2]

    def following(b):
        return b[0], b[1] + 1

    def chunk_before(b, c):
        return (b, c - 1) if c else ((b[0], b[1] - 1), NC - 1)

    def run(engine, steps, prologue, tail):
        prologue()
        steps((0, 0), [0], False, True)
        with engine.Fori(0, B // 2 - 1) as i:
            for s in range(2):
                steps((i, s), range(1, NC), True, True)
                steps((i, s + 1), [0], True, True)
        i = B // 2 - 1
        steps((i, 0), range(1, NC), True, True)
        steps((i, 1), [0], True, False)
        steps((i, 1), range(1, NC), True, False)
        tail((i, 1))

    with ExitStack() as ctx:
        def sb(name, shape, dt=F32):
            return ctx.enter_context(nc.sbuf_tensor(name, shape, dt))

        def sem(name):
            return ctx.enter_context(nc.semaphore(name))

        mask = sb("mask", [P, JB, N], BF16)
        x_in = sb("x_in", [P, JB, F])
        x_cols = sb("x1_cols", [P, KB, N])
        wh = sb("wh", [P, 2, JB, F + 2])
        s_fifth = sb("s_fifth", [P, 2, JB])
        s_row = sb("s_row", [P, N])
        best = sb("best", [P, 2, N])
        low = sb("low", [P, 2, N])
        e = sb("e", [P, ERING, CW])
        w_ext = sb("w_ext", [P, KB, F + 1])
        wa1 = sb("wa1", [P, KB])
        wa1_b = sb("wa1_b", [P, KB, P])
        a1_r = sb("a1_r", [P, F])
        a2_r = sb("a2_r", [P, F])
        x_res = sb("x_res", [P, 2, T, F])
        ident = sb("ident", [P, P])
        rden = sb("rden", [P, 2, T])
        h = sb("h", [P, 2, T, F])
        neg = sb("neg", [P, T, F])
        trash = neg
        bn = sb("bn1", [P, T, 6])
        mv = sb("mv1", [P, T, 2])
        var_eps = sb("var_eps1", [P, T])
        tick = sb("tick1", [P, 1])
        pool_tick = sb("pool_tick", [P, 1])
        minus_half = sb("minus_half1", [P, T])
        rstd = sb("rstd1", [P, T])
        nmr = sb("nmr1", [P, T])
        stage = e[:, :, :].rearrange("p (s a) i -> p s (a i)", s=2).bitcast(I32)

        prep_ps = ctx.enter_context(nc.psum_tensor("prep_ps", [P, 2, CW], F32))
        out_ps = ctx.enter_context(nc.psum_tensor("out_ps", [P, OUT_BANKS, CW], F32))

        s_w = sem("b_weights_loaded")
        s_adj = [sem(f"b_adj_loaded{i}") for i in range(2)]
        s_mask = sem("mask_made")
        s_diag = sem("diagonal_set")
        s_id = sem("identity_made")
        s_wa = sem("wa_made")
        s_x = sem("x1_loaded")
        s_xr = [sem("x1_chunk_loaded0"), sem("x1_chunk_loaded1")]
        s_prep = sem("prep_filled")
        s_prepread = sem("prep_read")
        s_fifths = sem("s_fifth_made")
        s_best = sem("best_updated")
        s_all = sem("best_reduced")
        s_rows = sem("rows_made")
        s_lin = sem("low_side_ready")
        s_max = sem("larger_side_taken")
        s_log = sem("logits_masked")
        s_e = sem("exp_ready")
        s_mm = sem("products_added")
        s_out = sem("chunk_summed")
        s_rd = sem("denominators_inverted")
        s_h = sem("h_scaled")
        s_min = sem("h_below_zero")
        s_en = sem("h_exp")
        s_elu = sem("elu_made")
        s_r = sem("residual_added")
        s_bn = sem("b_stats")
        s_ag = sem("b_mean_var")
        s_ve = sem("b_var_eps")
        s_pw = sem("b_rstd")
        s_rs = sem("b_nmr")
        s_y = sem("out_normed")
        s_st = [sem("out_stored0"), sem("out_stored1")]

        adj_v = adjT.rearrange("(q a p) (c i) -> c q p a i", p=P, a=4, i=CW)

        block = ctx.enter_context(nc.Block())

        @block.sync
        def _(sp):
            sp.dma_start(w_ext[:, :, 1:F + 1], W.rearrange("(k p) o -> p k o", p=P)).then_inc(s_w, 16)
            for r, i in ((a1_r, 0), (a2_r, 1)):
                sp.dma_start(r[:, :], a.rearrange("(s o) one -> s (o one)", s=2)[i].partition_broadcast(P))\
                  .then_inc(s_w, 16)
            def load_x(b):
                sp.dma_start(x_in[:, :, :], of_batch(x1, b).rearrange("(j p) f -> p j f", p=P)).then_inc(s_x, 16)

            def load_chunk(b, c):
                sp.dma_start(x_res[:, c % 2, :, :], of_batch(x1, b)[c * CW:(c + 1) * CW, :]
                             .rearrange("(t p) f -> p t f", p=P)).then_inc(s_xr[c % 2], 16)

            def store_chunk(b, c):
                sp.wait_ge(s_y, count(b, NC * T, T * (c + 1)))
                sp.dma_start(of_batch(out, b)[c * CW:(c + 1) * CW, :].rearrange("(t p) f -> p t f", p=P),
                             h[:, c % 2, :, :]).then_inc(s_st[c % 2], 16)

            def prologue():
                load_x((0, 0))
                for i in range(NC * 4):
                    if i >= 2:
                        sp.wait_ge(s_mask, i - 1)
                    sp.dma_start(stage[:, i % 2, :].rearrange("p (a i) -> p a i", a=4),
                                 adj_v[i % NC, i // NC]).then_inc(s_adj[i % 2], 16)
                load_chunk((0, 0), 0)
                load_chunk((0, 0), 1)
                sp.wait_ge(s_prep, TU)
                load_x((0, 1))

            def steps(b, chunks, prev, more):
                for c in chunks:
                    if c == 1 and more and not (isinstance(b[0], int) and 2 * b[0] + b[1] + 2 >= B):
                        sp.wait_ge(s_prep, count(following(b), USES, TU))
                        load_x((b[0], b[1] + 2))
                    if not prev:
                        continue
                    before = chunk_before(b, c)
                    store_chunk(*before)
                    if more or c + 1 < NC:
                        sp.wait_ge(s_r, count(before[0], NC, before[1] + 1))
                        load_chunk(*((b, c + 1) if c + 1 < NC else (following(b), 0)))

            def tail(b):
                store_chunk(b, NC - 1)
                for s in s_st:
                    sp.wait_ge(s, 16 + 16 * B * NC // 2)

            run(sp, steps, prologue, tail)

        @block.gpsimd
        def _(pool):
            pool.memset(ident[:, :], 0.0).then_inc(s_id, 1)
            pool.memset(wh[:, :, :, F + 1:F + 2], 1.0).then_inc(s_id, 1)
            pool.memset(minus_half[:, :], -0.5).then_inc(s_id, 1)
            pool.wait_ge(s_id, 3)
            pool.affine_select(out=ident[:, :], in_=ident[:, :], compare_op=ALU.not_equal, fill=1.0,
                               base=0, pattern=[[-1, P]], channel_multiplier=1).then_inc(s_id, 1)

            def reduce(b):
                p = b[1] % 2
                pool.wait_ge(s_best, count(b, JB, JB))
                pool.tensor_tensor(pool_tick[:, :], minus_half[:, 0:1], minus_half[:, 1:2], ALU.add)
                pool.partition_all_reduce(low[:, p, :], best[:, p, :], P, bass.bass_isa.ReduceOp.max)\
                    .then_inc(s_all, 1)

            def inverse_deviation(b, c):
                pool.wait_ge(s_ve, count(b, NC, c + 1))
                pool.tensor_tensor(rstd[:, :], var_eps[:, :], minus_half[:, :], ALU.pow).then_inc(s_pw, 1)

            def prologue():
                for j in range(JB):
                    if j % 4 == 0:
                        pool.wait_ge(s_mask, NC * (j // 4 + 1))
                    diag = mask[:, j, j * P:(j + 1) * P]
                    pool.affine_select(out=diag, in_=diag, compare_op=ALU.not_equal, fill=0.0,
                                       base=0, pattern=[[-1, P]], channel_multiplier=1).then_inc(s_diag, 1)
                reduce((0, 0))

            def steps(b, chunks, prev, more):
                for c in chunks:
                    if c == NC - 1 and more:
                        reduce(following(b))
                    if prev:
                        inverse_deviation(*chunk_before(b, c))

            run(pool, steps, prologue, lambda b: inverse_deviation(b, NC - 1))

        def bank(c, t):
            return (4 * (c % 2) + t) if t < 2 else t

        BANK_ORDER = (2, 3, 0, 1)

        @block.scalar
        def _(act):
            act.sem_inc(s_prepread, 2)
            act.preload_act_table_set("exp_and_others")
            act.wait_ge(s_w, 48)

            def take(b, u):
                p = b[1] % 2
                act.wait_ge(s_prep, count(b, USES, u + 1))
                if u < TU:
                    dst = x_cols[:, u // NC, (u % NC) * CW:(u % NC + 1) * CW]
                    src = prep_ps[:, u % 2, :]
                elif u < TU + SU:
                    c = u - TU
                    dst = s_row[:, c * CW:(c + 1) * CW]
                    src = prep_ps[:, u % 2, :]
                else:
                    dst = wh[:, p, u - TU - SU, 0:F + 1]
                    src = prep_ps[:, u % 2, 0:F + 1]
                act.activation(dst, src, ACT.Copy).then_inc(s_prepread, 1)

            def low_side(b, n):
                c, j = divmod(n, JB)
                p = b[1] % 2
                if n == 0:
                    act.wait_ge(s_rows, count(b, 4, 4))
                    act.wait_ge(s_fifths, count(b, 1, 1))
                act.wait_ge(s_mm, count(b, STEPS, n + 1))
                act.activation(e[:, n % ERING, :], low[:, p, c * CW:(c + 1) * CW], ACT.Identity,
                               bias=s_fifth[:, p, j:j + 1]).then_inc(s_lin, 1)

            def scale_h(b, c):
                act.wait_ge(s_st[c % 2], count(b, 16 * (NC // 2), 16 * (c // 2 + 1)))
                for k, t in enumerate(BANK_ORDER):
                    act.wait_ge(s_rd, count(b, NC * T, T * c + k + 1))
                    act.activation(h[:, c % 2, t, :], out_ps[:, bank(c, t), 0:F], ACT.Identity,
                                   scale=rden[:, c % 2, t:t + 1]).then_inc(s_h, 1)

            def exp_h(b, c):
                act.wait_ge(s_min, count(b, NC, c + 1))
                act.activation(neg[:, :, :], neg[:, :, :], ACT.Exp).then_inc(s_en, 1)

            def norm_h(b, c, t):
                if t == 0:
                    act.wait_ge(s_rs, count(b, NC, c + 1))
                act.activation(h[:, c % 2, t, :], h[:, c % 2, t, :], ACT.Identity,
                               scale=rstd[:, t:t + 1], bias=nmr[:, t:t + 1]).then_inc(s_y, 1)

            def prologue():
                for u in range(USES):
                    take((0, 0), u)
                for n in range(AHEAD):
                    low_side((0, 0), n)

            def steps(b, chunks, prev, more):
                for c in chunks:
                    before = chunk_before(b, c)
                    for j in range(JB):
                        n = c * JB + j
                        if n + AHEAD < STEPS:
                            low_side(b, n + AHEAD)
                        elif more:
                            low_side(following(b), n + AHEAD - STEPS)
                        act.wait_ge(s_log, count(b, STEPS, n + 1))
                        act.activation(e[:, n % ERING, :], e[:, n % ERING, :], ACT.Exp).then_inc(s_e, 1)
                        if more and 0 <= n - ACT_AT < USES:
                            take(following(b), n - ACT_AT)
                        if prev and j == 3:
                            scale_h(*before)
                        if prev and j == 6:
                            exp_h(*before)
                        if prev and 12 <= j < 12 + T:
                            norm_h(*before, j - 12)

            def tail(b):
                scale_h(b, NC - 1)
                exp_h(b, NC - 1)
                for t in range(T):
                    norm_h(b, NC - 1, t)

            run(act, steps, prologue, tail)

        @block.tensor
        def _(pe):
            pe.sem_inc(s_mm, ERING)
            pe.wait_ge(s_id, 4)
            pe.wait_ge(s_wa, 2 * KB + KB)

            def prepare(b, u):
                if u == 0:
                    pe.wait_ge(s_x, count(b, 16, 16))
                pe.wait_ge(s_prepread, count(b, USES, u + 1))
                if u < TU:
                    k, g = divmod(u, NC)
                    for t in range(T):
                        last = pe.transpose(prep_ps[:, u % 2, t * P:(t + 1) * P],
                                            x_in[:, g * T + t, k * P:(k + 1) * P], ident[:, :])
                elif u < TU + SU:
                    if u == TU:
                        pe.wait_ge(s_prepread, count(b, USES, 2 + TU))
                    c = u - TU
                    for k in range(KB):
                        last = pe.matmul(prep_ps[:, u % 2, :], wa1_b[:, k, :],
                                         x_cols[:, k, c * CW:(c + 1) * CW],
                                         start=(k == 0), stop=(k == KB - 1))
                else:
                    j = u - TU - SU
                    for k in range(KB):
                        last = pe.matmul(prep_ps[:, u % 2, 0:F + 1], x_cols[:, k, j * P:(j + 1) * P],
                                         w_ext[:, k, :], start=(k == 0), stop=(k == KB - 1))
                last.then_inc(s_prep, 1)

            def prologue():
                for u in range(USES):
                    prepare((0, 0), u)

            def steps(b, chunks, prev, more):
                p = b[1] % 2
                for c in chunks:
                    for j in range(JB):
                        n = c * JB + j
                        if n == 0:
                            pe.wait_ge(s_prepread, count(b, USES, 2 + USES))
                        pe.wait_ge(s_e, count(b, STEPS, n + 1))
                        for t in range(T):
                            if j == 0 and t == 0:
                                pe.wait_ge(s_h, count(b, NC * T, 2 * T + T * (c - 2) + T))
                            if j == 0 and t == 2:
                                pe.wait_ge(s_h, count(b, NC * T, 2 * T + T * (c - 1) + 2))
                            last = pe.matmul(out_ps[:, bank(c, t), 0:F + 1],
                                             e[:, n % ERING, t * P:(t + 1) * P], wh[:, p, j, 1:F + 2],
                                             start=(j == 0), stop=(j == JB - 1))
                        last.then_inc(s_mm, 1)
                        if more and 0 <= n - PE_AT < USES:
                            prepare(following(b), n - PE_AT)

            run(pe, steps, prologue, lambda b: None)

        @block.vector
        def _(dve):
            dve.sem_inc(s_h, 2 * T)
            for s in s_st:
                dve.sem_inc(s, 16)
            dve.wait_ge(s_w, 48)
            for k in range(KB):
                for i, (row, dst) in enumerate(((a1_r, wa1[:, k:k + 1]), (a2_r, w_ext[:, k, 0:1]))):
                    dve.tensor_tensor_reduce(out=trash[:, 2 * k + i, :], in0=w_ext[:, k, 1:F + 1], in1=row[:, :],
                                             scale=1.0, scalar=0.0, op0=ALU.mult, op1=ALU.add,
                                             accum_out=dst).then_inc(s_wa, 1)
            dve.wait_ge(s_wa, 2 * KB)
            dve.wait_ge(s_id, 1)
            for k in range(KB):
                dve.tensor_scalar(wa1_b[:, k, :], a1_r[:, 0:P], 0.0, wa1[:, k:k + 1], ALU.mult, ALU.add)\
                   .then_inc(s_wa, 1)

            def mask_piece(i):
                q, c = divmod(i, NC)
                dve.wait_ge(s_adj[i % 2], 16 * (i // 2 + 1))
                dve.tensor_scalar(mask[:, 4 * q:4 * q + 4, c * CW:(c + 1) * CW],
                                  stage[:, i % 2, :].rearrange("p (a i) -> p a i", a=4),
                                  0, -BIG, ALU.is_le, ALU.mult).then_inc(s_mask, 1)

            def fifths(b):
                p = b[1] % 2
                dve.wait_ge(s_prepread, count(b, USES, 2 + USES))
                dve.tensor_scalar(s_fifth[:, p, :], wh[:, p, :, 0], ALPHA, None, ALU.mult)\
                   .then_inc(s_fifths, 1)

            def maximum(b, j):
                p = b[1] % 2
                dve.wait_ge(s_prepread, count(b, USES, 2 + TU + SU + j + 1))
                if j == 0:
                    dve.tensor_scalar(best[:, p, :], mask[:, 0, :], wh[:, p, 0, 0:1], None, ALU.add)\
                       .then_inc(s_best, 1)
                else:
                    dve.wait_ge(s_best, count(b, JB, j))
                    dve.scalar_tensor_tensor(out=best[:, p, :], in0=mask[:, j, :], scalar=wh[:, p, j, 0:1],
                                             in1=best[:, p, :], op0=ALU.add, op1=ALU.max).then_inc(s_best, 1)

            def row_operation(b, k):
                p = b[1] % 2
                if k == 0:
                    dve.wait_ge(s_all, count(b, 1, 1))
                    dve.tensor_tensor(low[:, p, :], low[:, p, :], s_row[:, :], ALU.add).then_inc(s_rows, 1)
                if k == 1:
                    dve.wait_ge(s_rows, count(b, 4, 1))
                    dve.scalar_tensor_tensor(out=low[:, p, :], in0=low[:, p, :], scalar=ALPHA, in1=low[:, p, :],
                                             op0=ALU.mult, op1=ALU.max).then_inc(s_rows, 1)
                if k == 2:
                    dve.wait_ge(s_rows, count(b, 4, 2))
                    dve.tensor_tensor(best[:, p, :], s_row[:, :], low[:, p, :], ALU.subtract).then_inc(s_rows, 1)
                if k == 3:
                    dve.scalar_tensor_tensor(out=low[:, p, :], in0=s_row[:, :], scalar=ALPHA, in1=low[:, p, :],
                                             op0=ALU.mult, op1=ALU.subtract).then_inc(s_rows, 1)

            def invert(b, c):
                dve.wait_ge(s_mm, count(b, STEPS, ERING + (c + 1) * JB))
                for t in BANK_ORDER:
                    dve.reciprocal(rden[:, c % 2, t:t + 1], out_ps[:, bank(c, t), F:F + 1]).then_inc(s_rd, 1)

            def below_zero(b, c):
                dve.wait_ge(s_h, count(b, NC * T, 2 * T + T * (c + 1)))
                dve.tensor_scalar(neg[:, :, :], h[:, c % 2, :, :], 0.0, None, ALU.min).then_inc(s_min, 1)

            def elu(b, c):
                dve.wait_ge(s_en, count(b, NC, c + 1))
                dve.scalar_tensor_tensor(out=h[:, c % 2, :, :], in0=h[:, c % 2, :, :], scalar=0.0,
                                         in1=neg[:, :, :], op0=ALU.max, op1=ALU.add).then_inc(s_elu, 1)

            def residual(b, c):
                dve.wait_ge(s_elu, count(b, NC, c + 1))
                dve.wait_ge(s_xr[c % 2], count(b, 16 * (NC // 2), 16 * (c // 2 + 1)))
                dve.scalar_tensor_tensor(out=h[:, c % 2, :, :], in0=h[:, c % 2, :, :], scalar=-1.0,
                                         in1=x_res[:, c % 2, :, :], op0=ALU.add, op1=ALU.add)\
                   .then_inc(s_r, 1)

            def stats(b, c, t):
                dve.wait_ge(s_r, count(b, NC, c + 1))
                dve.bn_stats(bn[:, t, :], h[:, c % 2, t, :]).then_inc(s_bn, 1)

            def variance(b, c):
                dve.wait_ge(s_bn, count(b, NC * T, T * (c + 1)))
                dve.memset(tick[:, :], 0.0)
                for t in range(T):
                    dve.bn_aggr(mv[:, t, :], bn[:, t, :]).then_inc(s_ag, 1)
                dve.wait_ge(s_ag, count(b, NC * T, T * (c + 1)))
                dve.tensor_scalar(var_eps[:, :], mv[:, :, 1], EPS, None, ALU.add).then_inc(s_ve, 1)

            def offset(b, c):
                dve.wait_ge(s_pw, count(b, NC, c + 1))
                dve.scalar_tensor_tensor(out=nmr[:, :], in0=mv[:, :, 0], scalar=-1.0, in1=rstd[:, :],
                                         op0=ALU.mult, op1=ALU.mult).then_inc(s_rs, 1)

            def prologue():
                for i in range(NC * 4):
                    mask_piece(i)
                    if i % NC == NC - 1 and i >= NC:
                        for j in range(4 * (i // NC - 1), 4 * (i // NC)):
                            dve.wait_ge(s_diag, j + 1)
                            maximum((0, 0), j)
                for j in range(JB - 4, JB):
                    dve.wait_ge(s_diag, j + 1)
                    maximum((0, 0), j)
                fifths((0, 0))
                for k in range(4):
                    row_operation((0, 0), k)
                dve.wait_ge(s_rows, 4)

            def steps(b, chunks, prev, more):
                p = b[1] % 2
                for c in chunks:
                    before = chunk_before(b, c)
                    for j in range(JB):
                        n = c * JB + j
                        tile = e[:, n % ERING, :]
                        if n == 0:
                            dve.wait_ge(s_rows, count(b, 4, 4))
                        dve.wait_ge(s_lin, count(b, STEPS, n + 1))
                        dve.scalar_tensor_tensor(out=tile, in0=best[:, p, c * CW:(c + 1) * CW],
                                                 scalar=wh[:, p, j, 0:1], in1=tile, op0=ALU.add, op1=ALU.max)\
                           .then_inc(s_max, 1)
                        dve.wait_ge(s_max, count(b, STEPS, n + 1))
                        dve.tensor_tensor(tile, tile, mask[:, j, c * CW:(c + 1) * CW], ALU.add)\
                           .then_inc(s_log, 1)
                        if prev and j == 3:
                            invert(*before)
                        if prev and j == 5:
                            below_zero(*before)
                        if prev and j == 7:
                            elu(*before)
                        if prev and j == 8:
                            residual(*before)
                        if prev and j == 9:
                            for t in range(T):
                                stats(*before, t)
                        if prev and j == 10:
                            variance(*before)
                        if prev and j == 12:
                            offset(*before)
                        if more:
                            for m in range(JB):
                                if n == max_at(m):
                                    maximum(following(b), m)
                            if n == max_at(JB - 1) + 1:
                                fifths(following(b))
                            if n >= ROWS_AT and n - ROWS_AT < 4:
                                row_operation(following(b), n - ROWS_AT)

            def tail(b):
                c = NC - 1
                invert(b, c)
                below_zero(b, c)
                elu(b, c)
                residual(b, c)
                for t in range(T):
                    stats(b, c, t)
                variance(b, c)
                offset(b, c)

            run(dve, steps, prologue, tail)


def build(nc, x, xT, adjT, wqT, wkT, wvT, woT, bq, bk, bv, bo, gamma, beta, W, a, out):
    x1 = nc.dram_tensor("x1", tuple(x.shape), F32, kind="Internal").ap()
    layer0(nc, x, xT, adjT, wqT, wkT, wvT, woT, bq, bk, bv, bo, gamma, beta, x1)
    layer1(nc, x1, adjT, W, a, out)


def kernel(x, adj, L0_gnn_Wq, L0_gnn_bq, L0_gnn_Wk, L0_gnn_bk, L0_gnn_Wv, L0_gnn_bv, L0_gnn_Wo, L0_gnn_bo,
           L0_gnn_gamma, L0_gnn_beta, L1_gnn_W, L1_gnn_a):
    import numpy as np
    import concourse.bacc as bacc
    from concourse.bass_utils import run_bass_kernel_spmd

    x = np.asarray(x)
    arrays = {
        "x": x, "xT": x.transpose(0, 2, 1), "adjT": np.asarray(adj).T,
        "wqT": np.asarray(L0_gnn_Wq).T, "wkT": np.asarray(L0_gnn_Wk).T,
        "wvT": np.asarray(L0_gnn_Wv).T, "woT": np.asarray(L0_gnn_Wo).T,
        "bq": np.asarray(L0_gnn_bq), "bk": np.asarray(L0_gnn_bk), "bv": np.asarray(L0_gnn_bv),
        "bo": np.asarray(L0_gnn_bo), "gamma": np.asarray(L0_gnn_gamma), "beta": np.asarray(L0_gnn_beta),
        "W": np.asarray(L1_gnn_W), "a": np.asarray(L1_gnn_a),
    }
    arrays = {name: np.ascontiguousarray(v) for name, v in arrays.items()}
    nc = bacc.Bacc("TRN2", target_bir_lowering=False, num_devices=1, dynamic_dma_scratch_size=8192)
    args = [nc.dram_tensor(f"in_{name}", v.shape, mybir.dt.from_np(v.dtype), kind="ExternalInput").ap()
            for name, v in arrays.items()]
    out = nc.dram_tensor("out_0", x.shape, F32, kind="ExternalOutput").ap()
    build(nc, *args, out)
    r = run_bass_kernel_spmd(nc, [{f"in_{name}": v for name, v in arrays.items()}], core_ids=[0])
    return r.results[0]["out_0"]
```

```python
from contextlib import ExitStack

import concourse.bass as bass
from concourse import mybir

ALU = mybir.AluOpType
ACT = mybir.ActivationFunctionType
F32 = mybir.dt.float32
F32R = mybir.dt.float32r
BF16 = mybir.dt.bfloat16
I32 = mybir.dt.int32
I8 = mybir.dt.int8

P = 128
HEADS = 4
CLIP = 10.0
EPS = 1e-5
ALPHA = 0.2
BIG = 1.0e38

CW = 512
RING = 8
LAG = 4
SEG = 256


def layer0(nc, x, xT, adjT, wqT, wkT, wvT, woT, bq, bk, bv, bo, gamma, beta, x1):
    B, N, F = x.shape
    KB = F // P
    DH = F // HEADS
    PAIRS = HEADS // 2
    JB = N // P
    NC = N // CW
    T = CW // P
    ROUNDS = NC * PAIRS
    STEPS = ROUNDS * JB
    HALF = P // 2
    LIM = CLIP * DH ** 0.5
    SJ = SEG // P
    SEGS = STEPS // SJ
    RSEGS = JB // SJ
    D_AT, I_AT, M_AT, A_AT = 5, 5, 7, 3
    VU = JB // 2
    assert SJ == 2 and NC == 4 and JB == 16 and B >= 2

    uses = {(0, 0): ("v", 5), (0, 1): ("k", 0, 1), (0, 3): ("v", 6), (0, 4): ("k", 1, 1), (0, 6): ("v", 7),
            (0, 7): ("k", 2, 1), (0, 9): ("k", 3, 1), (1, 0): ("q", 1, 0), (1, 6): ("q", 1, 1)}
    for c in range(1, NC):
        if c + 1 < NC:
            uses.update({(PAIRS * c + p, 0): ("q", c + 1, p) for p in range(PAIRS)})
    uses.update({(PAIRS * c, 11 + t): ("o", t) for c in range(NC) for t in range(T)})
    NEXT = {(6, 0): ("q", 0, 0), (6, 6): ("q", 0, 1), (7, 0): ("k", 0, 0), (7, 2): ("k", 1, 0),
            (7, 4): ("k", 2, 0), (7, 6): ("k", 3, 0), (7, 8): ("v", 0), (7, 10): ("v", 1), (7, 12): ("v", 2),
            (7, 14): ("v", 3), (7, 15): ("v", 4)}
    order = sorted([*uses, *NEXT])
    PRJ = len(order)
    FIRST = len(NEXT)
    LAST = B * PRJ

    def count(b, per, n=0):
        i, s = b
        return i * per + (s * per + n)

    def batch_of(d, b):
        return d[b[0] + b[1]] if b[1] else d[b[0]]

    def following(b):
        return b[0], b[1] + 1

    def back(b, n, per):
        return (b, n) if n >= 0 else ((b[0], b[1] - 1), n + per)

    def use_number(b, at, more):
        skipped = 0 if more else sum(other < at for other in NEXT)
        return count(b, PRJ, FIRST + order.index(at) - skipped)

    def run(engine, prologue, chunk, tail):
        prologue()
        for c in range(2):
            chunk((0, 0), c, c, True)
        with engine.Fori(0, B - 1) as i:
            for s, c in ((0, 2), (0, 3), (1, 0), (1, 1)):
                chunk((i, s), c, 2, True)
        for c in (2, 3):
            chunk((B - 1, 0), c, 2, False)
        tail((B - 1, 0))

    with ExitStack() as ctx:
        def sb(name, shape, dt=F32):
            return ctx.enter_context(nc.sbuf_tensor(name, shape, dt))

        def sem(name):
            return ctx.enter_context(nc.semaphore(name))

        clip_hi = sb("clip_hi", [P, JB, N], I8)
        x_cols = sb("x_cols", [P, KB, N])
        k_split = sb("k_split", [P, HEADS, N], F32R)
        v_rows = sb("v_rows", [P, JB, F])
        q_hi = sb("q_hi", [P, 2, HEADS, CW], F32R)
        q_lo = sb("q_lo", [P, 2, HEADS, CW], F32R)
        probs = sb("probs", [P, RING, 2, CW])
        psums = sb("psums", [P, 2, 2, CW])
        inv_den = sb("inv_den", [P, 2, CW])
        seg_ctx = sb("seg_ctx", [P, 2, CW])
        ctx_t = sb("ctx_t", [P, 2, PAIRS, CW])
        x_rows = sb("x_rows", [P, 2, T, F])
        res = sb("res", [P, 2, T, F])
        wq = sb("wq", [P, KB, F])
        wk = sb("wk", [P, KB, F])
        wv = sb("wv", [P, KB, F])
        wo = sb("wo", [P, KB, F])
        bq_c = sb("bq_c", [P, PAIRS])
        bk_c = sb("bk_c", [P, PAIRS])
        bv_r = sb("bv_r", [P, F])
        bo_r = sb("bo_r", [P, F])
        gamma_r = sb("gamma_r", [P, F])
        beta_r = sb("beta_r", [P, F])
        ones = sb("ones", [P, HALF])
        bn = sb("bn", [P, 2, T, 6])
        mv = sb("mv", [P, 2, T, 2])
        var_eps = sb("var_eps", [P, 2, T])
        tick = sb("tick", [P, 1])
        minus_half = sb("minus_half", [P, T])
        rstd = sb("rstd", [P, 2, T])
        nmr = sb("nmr", [P, 2, T])

        sc_ps = ctx.enter_context(nc.psum_tensor("sc_ps", [P, 2, 2, CW], F32))
        ctx_ps = ctx.enter_context(nc.psum_tensor("ctx_ps", [P, 2, CW], F32))
        den_ps = ctx.enter_context(nc.psum_tensor("den_ps", [P, CW], F32))
        prj_ps = ctx.enter_context(nc.psum_tensor("prj_ps", [P, CW], F32))

        s_w = sem("weights_loaded")
        s_adj = [sem(f"adj_loaded{i}") for i in range(4)]
        s_flag = sem("adj_flagged")
        s_ones = sem("ones_set")
        s_xT = sem("x_cols_loaded")
        s_x = [sem("x_rows_loaded0"), sem("x_rows_loaded1")]
        s_xfree = sem("x_rows_used")
        s_fill = sem("slot_filled")
        s_read = sem("slot_read")
        s_khi = sem("k_hi_ready")
        s_klo = sem("k_lo_ready")
        s_v = sem("v_ready")
        s_prj = sem("prj_filled")
        s_prjfree = sem("prj_read")
        s_qhi = sem("q_hi_ready")
        s_qlo = sem("q_lo_ready")
        s_exp = sem("probs_ready")
        s_pv = sem("context_added")
        s_pool = sem("segment_summed")
        s_den = sem("den_ready")
        s_ln = sem("den_logged")
        s_inv = sem("den_inverted")
        s_norm = sem("segment_normed")
        s_acc = sem("segment_added")
        s_xb = sem("x_plus_bo")
        s_xbeta = sem("x_plus_beta")
        s_bn = [sem("stats_1"), sem("stats_2")]
        s_ag = [sem("mean_var_1"), sem("mean_var_2")]
        s_ve = [sem("var_eps_1"), sem("var_eps_2")]
        s_pw = [sem("rstd_1"), sem("rstd_2")]
        s_rs = [sem("nmr_1"), sem("nmr_2")]
        s_n = [sem("normed_1"), sem("normed_2")]
        s_gam = sem("times_gamma")
        s_z = sem("plus_x")
        s_x1 = [sem("x1_stored0"), sem("x1_stored1")]

        def head_rows(hh):
            return slice(HALF * hh, HALF * hh + HALF)

        stage = probs[:, :, :, :].rearrange("p (s a) h i -> p s (a h i)", s=4).bitcast(I32)
        adj_v = adjT.rearrange("(q a p) (c i) -> c q p a i", p=P, a=4, i=CW)

        block = ctx.enter_context(nc.Block())

        @block.sync
        def _(sp):
            for w, d in ((wk, wkT), (wv, wvT), (wq, wqT), (wo, woT)):
                sp.dma_start(w[:, :, :], d.rearrange("(k p) o -> p k o", p=P)).then_inc(s_w, 16)
            sp.dma_start(x_cols[:, :, :], xT[0].rearrange("(k p) n -> p k n", p=P)).then_inc(s_xT, 16)
            for i in range(NC * 4):
                if i >= 4:
                    sp.wait_ge(s_flag, 2 * (i - 3))
                sp.dma_start(stage[:, i % 4, :].rearrange("p (a i) -> p a i", a=4),
                             adj_v[i // 4, i % 4]).then_inc(s_adj[i % 4], 16)

            def load_rows(b, c):
                sp.wait_ge(s_xfree, count(b, NC, c + 1))
                sp.dma_start(x_rows[:, c % 2, :, :], batch_of(x, b)[c * CW:(c + 1) * CW, :]
                             .rearrange("(t p) f -> p t f", p=P)).then_inc(s_x[c % 2], 16)

            def store_x1(b, c):
                sp.wait_ge(s_n[1], count(b, NC * T, (c + 1) * T))
                sp.dma_start(batch_of(x1, b)[c * CW:(c + 1) * CW, :].rearrange("(t p) f -> p t f", p=P),
                             res[:, c % 2, :, :]).then_inc(s_x1[c % 2], 16)

            def chunk(b, c, prev, more):
                if prev == 2:
                    store_x1(*back(b, c - 2, NC))
                load_rows(b, c)
                if c == 2 and more:
                    sp.wait_ge(s_prj, use_number(b, (5, 0), more) + 1)
                    sp.dma_start(x_cols[:, :, :], batch_of(xT, following(b))
                                 .rearrange("(k p) n -> p k n", p=P)).then_inc(s_xT, 16)

            def tail(b):
                store_x1(b, NC - 2)
                store_x1(b, NC - 1)
                for s in s_x1:
                    sp.wait_ge(s, 16 + 16 * B * NC // 2)

            run(sp, lambda: None, chunk, tail)

        @block.gpsimd
        def _(pool):
            pool.memset(ones[:, :], 1.0).then_inc(s_ones, 1)
            pool.memset(minus_half[:, :], -0.5).then_inc(s_ones, 1)
            pool.wait_ge(s_ones, 2)
            pool.sem_inc(s_acc, 2)
            pool.sem_inc(s_pool, RING // SJ)

            def inverse_deviation(b, c, which):
                pool.wait_ge(s_ve[which], count(b, NC, c + 1))
                pool.tensor_tensor(rstd[:, which, :], var_eps[:, which, :], minus_half[:, :], ALU.pow)\
                    .then_inc(s_pw[which], 1)

            def add_segment(b, q):
                r, k = divmod(q, RSEGS)
                c, p = divmod(r, PAIRS)
                pool.wait_ge(s_norm, count(b, SEGS, 2 + q + 1))
                pool.wait_ge(s_acc, count(b, SEGS, 2 + q))
                if k == 0:
                    pool.sem_inc(s_acc, 1)
                    return
                pool.tensor_tensor(ctx_t[:, c % 2, p, :], ctx_t[:, c % 2, p, :], seg_ctx[:, q % 2, :],
                                   ALU.add).then_inc(s_acc, 1)

            def chunk(b, c, prev, more):
                for p in range(PAIRS):
                    for k in range(RSEGS):
                        q = (PAIRS * c + p) * RSEGS + k
                        pool.wait_ge(s_den, count(b, SEGS, q + 1))
                        pool.wait_ge(s_exp, count(b, STEPS, SJ * (q + 1)))
                        pool.tensor_tensor(psums[:, q % 2, :, :], probs[:, (SJ * q) % RING, :, :],
                                           probs[:, (SJ * q + 1) % RING, :, :], ALU.add).then_inc(s_pool, 1)
                        if prev or q >= A_AT:
                            add_segment(*back(b, q - A_AT, SEGS))
                        if k == 0 and p == 1 and prev:
                            inverse_deviation(*back(b, c - 1, NC), 0)
                        if k == 0 and p == 0 and prev == 2:
                            inverse_deviation(*back(b, c - 2, NC), 1)

            def tail(b):
                inverse_deviation(b, NC - 2, 1)
                for q in range(SEGS - A_AT, SEGS):
                    add_segment(b, q)
                inverse_deviation(b, NC - 1, 0)
                inverse_deviation(b, NC - 1, 1)

            run(pool, lambda: None, chunk, tail)

        @block.scalar
        def _(act):
            for t, d in ((bv_r, bv), (bo_r, bo), (gamma_r, gamma), (beta_r, beta)):
                act.dma_start(t[:, :], d.partition_broadcast(P)).then_inc(s_w, 16)
            with nc.allow_non_contiguous_dma(reason="256 biases, once"):
                act.dma_start(bq_c[:, :], bq.rearrange("(k p) -> p k", p=P)).then_inc(s_w, 16)
                act.dma_start(bk_c[:, :], bk.rearrange("(k p) -> p k", p=P)).then_inc(s_w, 16)
            act.preload_act_table_set("natural_log_exp_and_others")
            act.wait_ge(s_w, 160)

            def k_hi(c, p):
                for hh in range(2):
                    r = head_rows(hh)
                    act.activation(k_split[r, 2 * p + hh, c * CW:(c + 1) * CW], prj_ps[r, :], ACT.Identity,
                                   bias=bk_c[r, p:p + 1]).then_inc(s_khi, 1)

            def q_hi_part(c, p, k):
                hh, d = ((0, 0), (0, 1), (1, 1), (1, 0))[k]
                r = head_rows(hh)
                act.activation(q_hi[head_rows(d), c % 2, 2 * p + hh, :], prj_ps[r, :], ACT.Identity,
                               bias=bq_c[r, p:p + 1]).then_inc(s_qhi, 1)

            def norm(b, c, t, which):
                if t == 0:
                    act.wait_ge(s_rs[which], count(b, NC, c + 1))
                    if which == 1:
                        act.wait_ge(s_z, count(b, 2 * NC, 2 * c + 2))
                act.activation(res[:, c % 2, t, :], res[:, c % 2, t, :], ACT.Identity,
                               scale=rstd[:, which, t:t + 1], bias=nmr[:, which, t:t + 1])\
                   .then_inc(s_n[which], 1)

            def invert(b, q):
                act.wait_ge(s_den, count(b, SEGS, 2 + q + 1))
                act.wait_ge(s_norm, count(b, SEGS, q + 1))
                act.activation(inv_den[:, q % 2, :], den_ps[:, :], ACT.Ln).then_inc(s_ln, 1)
                act.wait_ge(s_ln, count(b, SEGS, 1 + q + 1))
                act.activation(inv_den[:, q % 2, :], inv_den[:, q % 2, :], ACT.Exp, scale=-1.0)\
                   .then_inc(s_inv, 1)

            def prologue():
                for u, at in enumerate(NEXT):
                    kind, *which = NEXT[at]
                    act.wait_ge(s_prj, u + 1)
                    if kind == "k":
                        k_hi(*which)
                    if kind == "q":
                        for k in range(4):
                            q_hi_part(*which, k)

            def chunk(b, c, prev, more):
                for r in (PAIRS * c, PAIRS * c + 1):
                    for j in range(JB):
                        p, n = r % PAIRS, r * JB + j
                        act.wait_ge(s_read, count(b, STEPS, 2 + n + 1))
                        act.activation(probs[:, n % RING, :, :], probs[:, n % RING, :, :], ACT.Exp,
                                       scale=DH ** -0.5).then_inc(s_exp, 1)
                        if (prev or n >= I_AT) and (n - I_AT) % SJ == 0:
                            at, m = back(b, n - I_AT, STEPS)
                            invert(at, m // SJ)
                        for later in range(2):
                            at = (r, j - later)
                            if at in uses or more and at in NEXT:
                                kind, *which = uses[at] if at in uses else NEXT[at]
                                if kind in "kq" and later == 0:
                                    act.wait_ge(s_prj, use_number(b, at, more) + 1)
                                if kind == "k" and later == 0:
                                    k_hi(*which)
                                if kind == "q":
                                    q_hi_part(*which, 2 * later)
                                    q_hi_part(*which, 2 * later + 1)
                        if prev and p == 1 and j in (6, 7, 8, 10):
                            norm(*back(b, c - 1, NC), (6, 7, 8, 10).index(j), 0)
                        if prev == 2 and p == 0 and j in (6, 8, 10, 12):
                            norm(*back(b, c - 2, NC), (6, 8, 10, 12).index(j), 1)

            def tail(b):
                for q in range((STEPS - I_AT + 1) // SJ, SEGS):
                    invert(b, q)
                for t in range(T):
                    norm(b, NC - 2, t, 1)
                for which in range(2):
                    for t in range(T):
                        norm(b, NC - 1, t, which)

            run(act, prologue, chunk, tail)

        @block.tensor
        def _(pe):
            pe.sem_inc(s_pv, RING)
            pe.sem_inc(s_den, 2)
            pe.sem_inc(s_ln, 1)
            pe.wait_ge(s_w, 160)
            pe.wait_ge(s_ones, 1)

            def project(b, kind, which, number):
                pe.wait_ge(s_prjfree, number + 1)
                if kind == "k":
                    c, p = which
                    for k in range(KB):
                        last = pe.matmul(prj_ps[:, :], wk[:, k, p * P:(p + 1) * P],
                                         x_cols[:, k, c * CW:(c + 1) * CW], start=(k == 0), stop=(k == KB - 1))
                if kind == "q":
                    c, p = which
                    for k in range(KB):
                        last = pe.matmul(prj_ps[:, :], wq[:, k, p * P:(p + 1) * P],
                                         x_cols[:, k, c * CW:(c + 1) * CW], start=(k == 0), stop=(k == KB - 1))
                if kind == "v":
                    g, = which
                    for t in range(2):
                        for k in range(KB):
                            last = pe.matmul(prj_ps[:, t * F:(t + 1) * F],
                                             x_cols[:, k, (2 * g + t) * P:(2 * g + t + 1) * P], wv[:, k, :],
                                             start=(k == 0), stop=(k == KB - 1))
                if kind == "o":
                    (at, c), t = b, which[0]
                    if t == 0:
                        pe.wait_ge(s_acc, count(at, SEGS, 2 + PAIRS * RSEGS * (c + 1)))
                    for k in range(KB):
                        last = pe.matmul(prj_ps[:, 0:F], ctx_t[:, c % 2, k, t * P:(t + 1) * P], wo[:, k, :],
                                         start=(k == 0), stop=(k == KB - 1))
                last.then_inc(s_prj, 1)

            def scores(b, n):
                r, j = divmod(n, JB)
                c, p = divmod(r, PAIRS)
                if j == 0:
                    pe.wait_ge(s_qlo, count(b, 8 * NC, 8 * c + 4 * (p + 1)))
                    pe.wait_ge(s_qhi, count(b, 8 * NC, 8 * c + 4 * (p + 1)))
                    if c == 0:
                        pe.wait_ge(s_khi, count(b, 4 * NC, 2 * NC * (p + 1)))
                        pe.wait_ge(s_klo, count(b, 4 * NC, 2 * NC * (p + 1)))
                pe.wait_ge(s_read, count(b, STEPS, n + 1))
                for hh in range(2):
                    h = 2 * p + hh
                    lhs = k_split[:, h, j * P:(j + 1) * P]
                    pe.matmul(sc_ps[:, n % 2, hh, :], lhs, q_hi[:, c % 2, h, :], start=True, stop=False)
                    last = pe.matmul(sc_ps[:, n % 2, hh, :], lhs, q_lo[:, c % 2, h, :],
                                     start=False, stop=True)
                last.then_inc(s_fill, 1)

            def context(b, n):
                r, j = divmod(n, JB)
                p, q = r % PAIRS, n // SJ
                if r == 0 and j % 2 == 0:
                    pe.wait_ge(s_v, count(b, VU, j // 2 + 1))
                if n % SJ == 0:
                    pe.wait_ge(s_norm, count(b, SEGS, q + 1))
                pe.wait_ge(s_exp, count(b, STEPS, n + 1))
                for hh in range(2):
                    h = 2 * p + hh
                    last = pe.matmul(ctx_ps[head_rows(hh), q % 2, :], v_rows[:, j, h * DH:(h + 1) * DH],
                                     probs[:, n % RING, hh, :], start=(n % SJ == 0), stop=(n % SJ == SJ - 1))
                last.then_inc(s_pv, 1)

            def denominator(b, q):
                pe.wait_ge(s_pool, count(b, SEGS, RING // SJ + q + 1))
                pe.wait_ge(s_ln, count(b, SEGS, q + 1))
                for hh in range(2):
                    last = pe.matmul(den_ps[head_rows(hh), :], ones[:, :], psums[:, q % 2, hh, :],
                                     start=True, stop=True)
                last.then_inc(s_den, 1)

            def prologue():
                pe.wait_ge(s_xT, 16)
                for u, at in enumerate(NEXT):
                    kind, *which = NEXT[at]
                    project(None, kind, which, u)

            def chunk(b, c, prev, more):
                for r in (PAIRS * c, PAIRS * c + 1):
                    for j in range(JB):
                        n = r * JB + j
                        scores(b, n)
                        if prev or n >= LAG:
                            context(*back(b, n - LAG, STEPS))
                        if (prev or n >= D_AT) and (n - D_AT) % SJ == 0:
                            at, m = back(b, n - D_AT, STEPS)
                            denominator(at, m // SJ)
                        at = (r, j)
                        if at in NEXT and more:
                            kind, *which = NEXT[at]
                            if at == (6, 0):
                                pe.wait_ge(s_xT, count(b, 16, 32))
                            project(b, kind, which, use_number(b, at, more))
                        if at in uses:
                            kind, *which = uses[at]
                            if kind != "o":
                                project(b, kind, which, use_number(b, at, more))
                            elif prev:
                                project(back(b, c - 1, NC), kind, which, use_number(b, at, more))
                            elif which[0] == 0:
                                pe.wait_ge(s_prjfree, use_number(b, at, more) + 1)
                                pe.sem_inc(s_prj, T)

            def tail(b):
                for n in range(STEPS - LAG, STEPS):
                    context(b, n)
                for q in range((STEPS - D_AT + 1) // SJ, SEGS):
                    denominator(b, q)
                for t in range(T):
                    project((b, NC - 1), "o", (t,), LAST + t)

            run(pe, prologue, chunk, tail)

        @block.vector
        def _(dve):
            dve.sem_inc(s_read, 2)
            dve.sem_inc(s_prjfree, 1)
            dve.sem_inc(s_norm, 2)
            dve.sem_inc(s_xfree, 2)
            for s in s_x1:
                dve.sem_inc(s, 16)
            def k_lo(b, c, p):
                dve.wait_ge(s_khi, count(b, 4 * NC, 2 * NC * p + 2 * (c + 1)))
                for hh in range(2):
                    r, o, h = head_rows(hh), head_rows(1 - hh), 2 * p + hh
                    dve.scalar_tensor_tensor(
                        out=k_split[o, h, c * CW:(c + 1) * CW], in0=prj_ps[r, :], scalar=bk_c[r, p:p + 1],
                        in1=k_split[r, h, c * CW:(c + 1) * CW].bitcast(F32),
                        op0=ALU.add, op1=ALU.subtract).then_inc(s_klo, 1)
                dve.wait_ge(s_klo, count(b, 4 * NC, 2 * NC * p + 2 * (c + 1)))
                dve.sem_inc(s_prjfree, 1)

            def q_lo_part(b, c, p, k):
                hh, d = ((0, 0), (0, 1), (1, 1), (1, 0))[k]
                r = head_rows(hh)
                if k == 0:
                    dve.wait_ge(s_qhi, count(b, 8 * NC, 8 * c + 4 * (p + 1)))
                dve.scalar_tensor_tensor(out=q_lo[head_rows(d), c % 2, 2 * p + hh, :], in0=prj_ps[r, :],
                                         scalar=bq_c[r, p:p + 1],
                                         in1=q_hi[r, c % 2, 2 * p + hh, :].bitcast(F32),
                                         op0=ALU.add, op1=ALU.subtract).then_inc(s_qlo, 1)
                if k == 3:
                    dve.wait_ge(s_qlo, count(b, 8 * NC, 8 * c + 4 * (p + 1)))
                    dve.sem_inc(s_prjfree, 1)

            def take_v(b, g, number):
                dve.wait_ge(s_prj, number + 1)
                dve.tensor_tensor(v_rows[:, 2 * g:2 * g + 2, :],
                                  prj_ps[:, :].rearrange("p (t f) -> p t f", f=F),
                                  bv_r[:, None, :].broadcast_to([P, 2, F]), ALU.add).then_inc(s_v, 1)
                dve.wait_ge(s_v, count(b, VU, g + 1))
                dve.sem_inc(s_prjfree, 1)

            def normalise(b, q):
                r, k = divmod(q, RSEGS)
                c, p = divmod(r, PAIRS)
                dve.wait_ge(s_inv, count(b, SEGS, q + 1))
                dve.wait_ge(s_pv, count(b, STEPS, RING + SJ * (q + 1)))
                if k == 0:
                    to = ctx_t[:, c % 2, p, :]
                else:
                    dve.wait_ge(s_acc, count(b, SEGS, q + 1))
                    to = seg_ctx[:, q % 2, :]
                dve.tensor_tensor(to, ctx_ps[:, q % 2, :], inv_den[:, q % 2, :], ALU.mult).then_inc(s_norm, 1)

            def add_bo(b, c, half):
                two = slice(2 * half, 2 * half + 2)
                if half == 0:
                    dve.wait_ge(s_x[c % 2], count(b, 16 * (NC // 2), 16 * (c // 2 + 1)))
                    dve.wait_ge(s_x1[c % 2], count(b, 16 * (NC // 2), 16 * (c // 2 + 1)))
                dve.tensor_tensor(res[:, c % 2, two, :], x_rows[:, c % 2, two, :],
                                  bo_r[:, None, :].broadcast_to([P, 2, F]), ALU.add).then_inc(s_xb, 1)

            def add_beta(b, c, half):
                two = slice(2 * half, 2 * half + 2)
                dve.wait_ge(s_xb, count(b, 2 * NC, 2 * c + 2))
                dve.tensor_tensor(x_rows[:, c % 2, two, :], x_rows[:, c % 2, two, :],
                                  beta_r[:, None, :].broadcast_to([P, 2, F]), ALU.add).then_inc(s_xbeta, 1)

            def add_projection(b, c, t, number):
                dve.wait_ge(s_prj, number + 1)
                dve.wait_ge(s_xb, count(b, 2 * NC, 2 * c + 2))
                dve.tensor_tensor(res[:, c % 2, t, :], prj_ps[:, 0:F], res[:, c % 2, t, :], ALU.add)\
                   .then_inc(s_prjfree, 1)
                dve.wait_ge(s_prjfree, 1 + number + 1)
                dve.bn_stats(bn[:, 0, t, :], res[:, c % 2, t, :]).then_inc(s_bn[0], 1)

            def stats(b, c, t):
                dve.wait_ge(s_z, count(b, 2 * NC, 2 * c + 1 + t // 2))
                dve.bn_stats(bn[:, 1, t, :], res[:, c % 2, t, :]).then_inc(s_bn[1], 1)

            def variance(b, c, which):
                dve.wait_ge(s_bn[which], count(b, NC * T, T * (c + 1)))
                dve.memset(tick[:, :], 0.0)
                for t in range(T):
                    dve.bn_aggr(mv[:, which, t, :], bn[:, which, t, :]).then_inc(s_ag[which], 1)
                dve.wait_ge(s_ag[which], count(b, NC * T, T * (c + 1)))
                dve.tensor_scalar(var_eps[:, which, :], mv[:, which, :, 1], EPS, None, ALU.add)\
                   .then_inc(s_ve[which], 1)

            def offset(b, c, which):
                dve.wait_ge(s_pw[which], count(b, NC, c + 1))
                dve.scalar_tensor_tensor(out=nmr[:, which, :], in0=mv[:, which, :, 0], scalar=-1.0,
                                         in1=rstd[:, which, :], op0=ALU.mult, op1=ALU.mult)\
                   .then_inc(s_rs[which], 1)

            def times_gamma(b, c, half):
                two = slice(2 * half, 2 * half + 2)
                dve.wait_ge(s_n[0], count(b, NC * T, T * c + 2 * (half + 1)))
                dve.tensor_tensor(res[:, c % 2, two, :], res[:, c % 2, two, :],
                                  gamma_r[:, None, :].broadcast_to([P, 2, F]), ALU.mult).then_inc(s_gam, 1)

            def add_x(b, c, half):
                two = slice(2 * half, 2 * half + 2)
                dve.wait_ge(s_gam, count(b, 2 * NC, 2 * c + 1 + half))
                dve.wait_ge(s_xbeta, count(b, 2 * NC, 2 * c + 1 + half))
                dve.tensor_tensor(res[:, c % 2, two, :], res[:, c % 2, two, :],
                                  x_rows[:, c % 2, two, :], ALU.add).then_inc(s_z, 1)
                if half == 1:
                    dve.wait_ge(s_z, count(b, 2 * NC, 2 * c + 2))
                    dve.sem_inc(s_xfree, 1)

            def clip_piece(i):
                c, q = divmod(i, 4)
                dve.wait_ge(s_adj[i % 4], 16 * (i // 4 + 1))
                piece = stage[:, i % 4, :]
                dve.tensor_scalar(piece, piece, 0, int(2 * LIM), ALU.not_equal, ALU.mult).then_inc(s_flag, 1)
                dve.wait_ge(s_flag, 2 * i + 1)
                dve.tensor_scalar(clip_hi[:, 4 * q:4 * q + 4, c * CW:(c + 1) * CW],
                                  piece.rearrange("p (a i) -> p a i", a=4), -LIM, None, ALU.add)\
                   .then_inc(s_flag, 1)

            def prologue():
                dve.wait_ge(s_w, 160)
                for i in range(NC * 4):
                    if i < FIRST:
                        kind, *which = NEXT[list(NEXT)[i]]
                        if kind == "k":
                            k_lo((0, 0), *which)
                        if kind == "q":
                            for k in range(4):
                                q_lo_part((0, 0), *which, k)
                        if kind == "v":
                            take_v((0, 0), *which, i)
                    clip_piece(i)
                dve.wait_ge(s_flag, 2 * NC * 4)

            def chunk(b, c, prev, more):
                for r in (PAIRS * c, PAIRS * c + 1):
                    for j in range(JB):
                        p, n = r % PAIRS, r * JB + j
                        dve.wait_ge(s_fill, count(b, STEPS, n + 1))
                        dve.wait_ge(s_pv, count(b, STEPS, n + 1))
                        if n % SJ == 0:
                            dve.wait_ge(s_pool, count(b, SEGS, n // SJ + 1))
                        dve.scalar_tensor_tensor(
                            out=probs[:, n % RING, :, :], in0=sc_ps[:, n % 2, :, :], scalar=-LIM,
                            in1=clip_hi[:, j, c * CW:(c + 1) * CW][:, None, :].broadcast_to([P, 2, CW]),
                            op0=ALU.max, op1=ALU.min).then_inc(s_read, 1)
                        if (prev or n >= M_AT) and (n - M_AT) % SJ == 0:
                            at, m = back(b, n - M_AT, STEPS)
                            normalise(at, m // SJ)
                        for later in (4, 2, 1, 0):
                            at = (r, j - later)
                            if at in uses or more and at in NEXT:
                                kind, *which = uses[at] if at in uses else NEXT[at]
                                of = b if at in uses and uses[at][0] in "kvq" else following(b)
                                if kind == "v" and later == 0:
                                    take_v(of, *which, use_number(b, at, more))
                                if kind == "k" and later == 1:
                                    k_lo(of, *which)
                                if kind == "q" and later >= 2:
                                    q_lo_part(of, *which, later - 2)
                                    q_lo_part(of, *which, later - 1)
                        before = back(b, c - 1, NC)
                        if prev and p == 0:
                            if j in (0, 1):
                                add_bo(*before, j)
                            if j == 5 and prev == 2:
                                offset(*back(b, c - 2, NC), 1)
                            if 11 <= j <= 14:
                                add_projection(*before, j - 11, use_number(b, (r, j), more))
                            if j == 15:
                                variance(*before, 0)
                        if not prev and (r, j) == (0, 12):
                            dve.sem_inc(s_prjfree, T)
                        if prev and p == 1:
                            if j in (0, 1):
                                add_beta(*before, j)
                            if j == 5:
                                offset(*before, 0)
                            if j in (9, 11):
                                times_gamma(*before, (j - 9) // 2)
                            if j in (10, 12):
                                add_x(*before, (j - 10) // 2)
                            if j in (13, 14):
                                stats(*before, 2 * (j - 13))
                                stats(*before, 2 * (j - 13) + 1)
                            if j == 15:
                                variance(*before, 1)

            def tail(b):
                c = NC - 1
                add_bo(b, c, 0)
                add_bo(b, c, 1)
                offset(b, c - 1, 1)
                add_beta(b, c, 0)
                add_beta(b, c, 1)
                for q in range((STEPS - M_AT + 1) // SJ, SEGS):
                    normalise(b, q)
                for t in range(T):
                    add_projection(b, c, t, LAST + t)
                variance(b, c, 0)
                offset(b, c, 0)
                for half in range(2):
                    times_gamma(b, c, half)
                for half in range(2):
                    add_x(b, c, half)
                for t in range(T):
                    stats(b, c, t)
                variance(b, c, 1)
                offset(b, c, 1)

            run(dve, prologue, chunk, tail)


def layer1(nc, x1, adjT, W, a, out):
    B, N, F = x1.shape
    KB = F // P
    JB = N // P
    NC = N // CW
    T = CW // P
    STEPS = NC * JB
    ERING = 8
    AHEAD = 3
    OUT_BANKS = 6
    TU, WU, SU = KB * NC, JB, NC
    USES = TU + WU + SU

    uses_at = [1 + u for u in range(TU)] + [10 + 27 * j // JB for j in range(JB)] \
        + [37 + 2 * c for c in range(NC)]
    TAKEN = 4
    assert len(uses_at) == USES and uses_at[-1] + TAKEN < STEPS - AHEAD

    def uses_in(n):
        return [u for u, at in enumerate(uses_at) if at == n]

    assert NC * T == JB and B % 2 == 0 and B >= 4

    LATE = 3

    ON_POOL = (5, 8, 10, 12, 13)
    ON_DVE = [j for j in range(JB) if j not in ON_POOL]

    def max_at(j):
        return 17 + 27 * j // JB

    ROWS_AT = (53, 55, 57, 59)

    def count(b, per, n=0):
        i, s = b
        return i * (2 * per) + (s * per + n)

    def of_batch(d, b):
        i, s = b
        return d.rearrange("(i s) n f -> i s n f", s=2)[i + s // 2, s % 2]

    def following(b):
        return b[0], b[1] + 1

    def chunk_before(b, c):
        return (b, c - 1) if c else ((b[0], b[1] - 1), NC - 1)

    def run(engine, steps, prologue, tail):
        prologue()
        steps((0, 0), [0], False, True)
        with engine.Fori(0, B // 2 - 1) as i:
            for s in range(2):
                steps((i, s), range(1, NC), True, True)
                steps((i, s + 1), [0], True, True)
        i = B // 2 - 1
        steps((i, 0), range(1, NC), True, True)
        steps((i, 1), [0], True, False)
        steps((i, 1), range(1, NC), True, False)
        tail((i, 1))

    with ExitStack() as ctx:
        def sb(name, shape, dt=F32):
            return ctx.enter_context(nc.sbuf_tensor(name, shape, dt))

        def sem(name):
            return ctx.enter_context(nc.semaphore(name))

        mask = sb("mask", [P, JB, N], BF16)
        x_in = sb("x_in", [P, JB, F])
        x_cols = sb("x1_cols", [P, KB, N])
        wh = sb("wh", [P, 2, JB, F + 2])
        s_fifth = sb("s_fifth", [P, 2, JB])
        s_row = sb("s_row", [P, N])
        best = sb("best", [P, 2, N])
        low = sb("low", [P, 2, N])
        e = sb("e", [P, ERING, CW])
        w_ext = sb("w_ext", [P, KB, F + 1])
        wa1 = sb("wa1", [P, KB])
        wa1_b = sb("wa1_b", [P, KB, P])
        a1_r = sb("a1_r", [P, F])
        a2_r = sb("a2_r", [P, F])
        x_res = sb("x_res", [P, 2, T, F])
        ident = sb("ident", [P, P])
        rden = sb("rden", [P, 2, T])
        h = sb("h", [P, 2, T, F])
        neg = sb("neg", [P, T, F])
        trash = neg
        bn = sb("bn1", [P, T, 6])
        mv = sb("mv1", [P, T, 2])
        var_eps = sb("var_eps1", [P, T])
        tick = sb("tick1", [P, 1])
        pool_tick = sb("pool_tick", [P, 1])
        minus_half = sb("minus_half1", [P, T])
        one = sb("one", [P, 1])
        rstd = sb("rstd1", [P, T])
        nmr = sb("nmr1", [P, T])
        halves = e[:, :, :].rearrange("p (s a) i -> p s (a i)", s=2).bitcast(I32)
        stages = [halves[:, 0, :], halves[:, 1, :],
                  h[:, :, :, :].rearrange("p s t f -> p (s t f)").bitcast(I32),
                  x_res[:, :, :, :].rearrange("p s t f -> p (s t f)").bitcast(I32)]

        prep_ps = ctx.enter_context(nc.psum_tensor("prep_ps", [P, 2, CW], F32))
        out_ps = ctx.enter_context(nc.psum_tensor("out_ps", [P, OUT_BANKS, CW], F32))

        s_w = sem("b_weights_loaded")
        s_adj = [sem(f"b_adj_loaded{i}") for i in range(4)]
        s_mask = sem("mask_made")
        s_diag = sem("diagonal_set")
        s_id = sem("identity_made")
        s_wa = sem("wa_made")
        s_x = sem("x1_loaded")
        s_xr = [sem("x1_chunk_loaded0"), sem("x1_chunk_loaded1")]
        s_prep = sem("prep_filled")
        s_prepread = sem("prep_read")
        s_fifths = sem("s_fifth_made")
        s_best = sem("best_updated")
        s_all = sem("best_reduced")
        s_rows = sem("rows_made")
        s_lin = sem("low_side_ready")
        s_max = sem("larger_side_taken")
        s_log = sem("logits_masked")
        s_logp = sem("logits_masked_by_pool")
        s_e = sem("exp_ready")
        s_mm = sem("products_added")
        s_rd = sem("denominators_inverted")
        s_h = sem("h_scaled")
        s_min = sem("h_below_zero")
        s_en = sem("h_exp")
        s_elu = sem("elu_made")
        s_x1r = sem("x1_less_one")
        s_r = sem("residual_added")
        s_bn = sem("b_stats")
        s_ag = sem("b_mean_var")
        s_ve = sem("b_var_eps")
        s_pw = sem("b_rstd")
        s_rs = sem("b_nmr")
        s_y = sem("out_normed")
        s_st = [sem("out_stored0"), sem("out_stored1")]

        adj_v = adjT.rearrange("(q a p) (c i) -> c q p a i", p=P, a=4, i=CW)

        block = ctx.enter_context(nc.Block())

        @block.sync
        def _(sp):
            sp.dma_start(w_ext[:, :, 1:F + 1], W.rearrange("(k p) o -> p k o", p=P)).then_inc(s_w, 16)
            for r, i in ((a1_r, 0), (a2_r, 1)):
                sp.dma_start(r[:, :], a.rearrange("(s o) one -> s (o one)", s=2)[i].partition_broadcast(P))\
                  .then_inc(s_w, 16)
            def load_x(b):
                sp.dma_start(x_in[:, :, :], of_batch(x1, b).rearrange("(j p) f -> p j f", p=P)).then_inc(s_x, 16)

            def load_chunk(b, c):
                sp.dma_start(x_res[:, c % 2, :, :], of_batch(x1, b)[c * CW:(c + 1) * CW, :]
                             .rearrange("(t p) f -> p t f", p=P)).then_inc(s_xr[c % 2], 16)

            def store_chunk(b, c):
                sp.wait_ge(s_y, count(b, NC * T, T * (c + 1)))
                sp.dma_start(of_batch(out, b)[c * CW:(c + 1) * CW, :].rearrange("(t p) f -> p t f", p=P),
                             h[:, c % 2, :, :]).then_inc(s_st[c % 2], 16)

            def prologue():
                load_x((0, 0))
                for i in range(NC * 4):
                    if i >= 4:
                        sp.wait_ge(s_mask, i - 3)
                    sp.dma_start(stages[i % 4].rearrange("p (a i) -> p a i", a=4),
                                 adj_v[i % NC, i // NC]).then_inc(s_adj[i % 4], 16)
                sp.wait_ge(s_mask, NC * 4)
                load_chunk((0, 0), 0)
                load_chunk((0, 0), 1)
                sp.wait_ge(s_prep, TU)
                load_x((0, 1))

            def steps(b, chunks, prev, more):
                for c in chunks:
                    if c == 1 and more and not (isinstance(b[0], int) and 2 * b[0] + b[1] + 2 >= B):
                        sp.wait_ge(s_prep, count(following(b), USES, TU))
                        load_x((b[0], b[1] + 2))
                    if not prev:
                        continue
                    before = chunk_before(b, c)
                    store_chunk(*before)
                    if more or c + 1 < NC:
                        sp.wait_ge(s_r, count(before[0], NC, before[1] + 1))
                        load_chunk(*((b, c + 1) if c + 1 < NC else (following(b), 0)))

            def tail(b):
                store_chunk(b, NC - 1)
                for s in s_st:
                    sp.wait_ge(s, 16 + 16 * B * NC // 2)

            run(sp, steps, prologue, tail)

        @block.gpsimd
        def _(pool):
            pool.memset(ident[:, :], 0.0).then_inc(s_id, 1)
            pool.memset(wh[:, :, :, F + 1:F + 2], 1.0).then_inc(s_id, 1)
            pool.memset(minus_half[:, :], -0.5).then_inc(s_id, 1)
            pool.memset(one[:, :], 1.0).then_inc(s_id, 1)
            pool.wait_ge(s_id, 4)
            pool.affine_select(out=ident[:, :], in_=ident[:, :], compare_op=ALU.not_equal, fill=1.0,
                               base=0, pattern=[[-1, P]], channel_multiplier=1).then_inc(s_id, 1)

            def reduce(b):
                p = b[1] % 2
                pool.wait_ge(s_best, count(b, JB, JB))
                pool.tensor_tensor(pool_tick[:, :], minus_half[:, 0:1], minus_half[:, 1:2], ALU.add)
                pool.partition_all_reduce(low[:, p, :], best[:, p, :], P, bass.bass_isa.ReduceOp.max)\
                    .then_inc(s_all, 1)

            def add_mask(b, c, j):
                n = c * JB + j
                tile = e[:, n % ERING, :]
                pool.wait_ge(s_max, count(b, STEPS, n + 1))
                pool.tensor_tensor(tile, tile, mask[:, j, c * CW:(c + 1) * CW], ALU.add).then_inc(s_logp, 1)

            def less_one(b, c):
                pool.wait_ge(s_xr[c % 2], count(b, 16 * (NC // 2), 16 * (c // 2 + 1)))
                pool.tensor_tensor(x_res[:, c % 2, :, :], x_res[:, c % 2, :, :],
                                   one[:, :, None].broadcast_to([P, T, F]), ALU.subtract).then_inc(s_x1r, 1)

            def residual(b, c):
                pool.wait_ge(s_elu, count(b, NC, c + 1))
                pool.wait_ge(s_x1r, count(b, NC, c + 1))
                pool.tensor_tensor(h[:, c % 2, :, :], h[:, c % 2, :, :], x_res[:, c % 2, :, :], ALU.add)\
                    .then_inc(s_r, 1)

            def inverse_deviation(b, c):
                pool.wait_ge(s_ve, count(b, NC, c + 1))
                pool.tensor_tensor(rstd[:, :], var_eps[:, :], minus_half[:, :], ALU.pow).then_inc(s_pw, 1)

            def prologue():
                for j in range(JB):
                    if j % 4 == 0:
                        pool.wait_ge(s_mask, NC * (j // 4 + 1))
                    diag = mask[:, j, j * P:(j + 1) * P]
                    pool.affine_select(out=diag, in_=diag, compare_op=ALU.not_equal, fill=0.0,
                                       base=0, pattern=[[-1, P]], channel_multiplier=1).then_inc(s_diag, 1)
                reduce((0, 0))

            def steps(b, chunks, prev, more):
                for c in chunks:
                    if c == NC - 1 and more:
                        reduce(following(b))
                    if prev:
                        less_one(*chunk_before(b, c))
                    for j in ON_POOL:
                        if j == 13 and prev:
                            inverse_deviation(*chunk_before(b, c))
                        add_mask(b, c, j)
                        if j == 5 and prev:
                            residual(*chunk_before(b, c))

            def tail(b):
                less_one(b, NC - 1)
                residual(b, NC - 1)
                inverse_deviation(b, NC - 1)

            run(pool, steps, prologue, tail)

        def bank(c, t):
            return (4 * (c % 2) + t) if t < 2 else t

        BANK_ORDER = (2, 3, 0, 1)

        @block.scalar
        def _(act):
            act.sem_inc(s_prepread, 2)
            act.preload_act_table_set("exp_and_others")
            act.wait_ge(s_w, 48)

            def take(b, u):
                p = b[1] % 2
                act.wait_ge(s_prep, count(b, USES, u + 1))
                if u < TU:
                    dst = x_cols[:, u // NC, (u % NC) * CW:(u % NC + 1) * CW]
                    src = prep_ps[:, u % 2, :]
                elif u < TU + WU:
                    dst = wh[:, p, u - TU, 0:F + 1]
                    src = prep_ps[:, u % 2, 0:F + 1]
                else:
                    c = u - TU - WU
                    dst = s_row[:, c * CW:(c + 1) * CW]
                    src = prep_ps[:, u % 2, :]
                act.activation(dst, src, ACT.Copy).then_inc(s_prepread, 1)

            def low_side(b, n):
                c, j = divmod(n, JB)
                p = b[1] % 2
                if n == 0:
                    act.wait_ge(s_rows, count(b, 4, 4))
                    act.wait_ge(s_fifths, count(b, 1, 1))
                act.wait_ge(s_mm, count(b, STEPS, n + 1))
                act.activation(e[:, n % ERING, :], low[:, p, c * CW:(c + 1) * CW], ACT.Identity,
                               bias=s_fifth[:, p, j:j + 1]).then_inc(s_lin, 1)

            def scale_h(b, c):
                act.wait_ge(s_st[c % 2], count(b, 16 * (NC // 2), 16 * (c // 2 + 1)))
                for k, t in enumerate(BANK_ORDER):
                    act.wait_ge(s_rd, count(b, NC * T, T * c + k + 1))
                    act.activation(h[:, c % 2, t, :], out_ps[:, bank(c, t), 0:F], ACT.Identity,
                                   scale=rden[:, c % 2, t:t + 1]).then_inc(s_h, 1)

            def exp_h(b, c):
                act.wait_ge(s_h, count(b, NC * T, 2 * T + T * (c + 1)))
                act.activation(neg[:, :, :], h[:, c % 2, :, :], ACT.Relu, scale=-1.0).then_inc(s_min, 1)
                act.wait_ge(s_min, count(b, NC, c + 1))
                act.activation(neg[:, :, :], neg[:, :, :], ACT.Exp, scale=-1.0).then_inc(s_en, 1)

            def norm_h(b, c, t):
                if t == 0:
                    act.wait_ge(s_rs, count(b, NC, c + 1))
                act.activation(h[:, c % 2, t, :], h[:, c % 2, t, :], ACT.Identity,
                               scale=rstd[:, t:t + 1], bias=nmr[:, t:t + 1]).then_inc(s_y, 1)

            def prologue():
                for u in range(USES):
                    take((0, 0), u)
                for n in range(AHEAD):
                    low_side((0, 0), n)

            def steps(b, chunks, prev, more):
                for c in chunks:
                    before = chunk_before(b, c)
                    for j in range(JB):
                        n = c * JB + j
                        if n + AHEAD < STEPS:
                            low_side(b, n + AHEAD)
                        elif more:
                            low_side(following(b), n + AHEAD - STEPS)
                        if j in ON_POOL:
                            act.wait_ge(s_logp, count(b, NC * len(ON_POOL),
                                                      c * len(ON_POOL) + ON_POOL.index(j) + 1))
                        else:
                            act.wait_ge(s_log, count(b, NC * len(ON_DVE), c * len(ON_DVE) + ON_DVE.index(j) + 1))
                        act.activation(e[:, n % ERING, :], e[:, n % ERING, :], ACT.Exp).then_inc(s_e, 1)
                        for u in uses_in(n - TAKEN) if more else ():
                            take(following(b), u)
                        if prev and j == 2:
                            scale_h(*before)
                        if prev and j == 4:
                            exp_h(*before)
                        if prev and 13 <= j < 13 + T // 2:
                            norm_h(*before, 2 * (j - 13))
                            norm_h(*before, 2 * (j - 13) + 1)

            def tail(b):
                scale_h(b, NC - 1)
                exp_h(b, NC - 1)
                for t in range(T):
                    norm_h(b, NC - 1, t)

            run(act, steps, prologue, tail)

        @block.tensor
        def _(pe):
            pe.sem_inc(s_mm, ERING)
            pe.wait_ge(s_id, 5)
            pe.wait_ge(s_wa, 2 * KB + KB)

            def prepare(b, u):
                if u == 0:
                    pe.wait_ge(s_x, count(b, 16, 16))
                pe.wait_ge(s_prepread, count(b, USES, u + 1))
                if u < TU:
                    k, g = divmod(u, NC)
                    for t in range(T):
                        last = pe.transpose(prep_ps[:, u % 2, t * P:(t + 1) * P],
                                            x_in[:, g * T + t, k * P:(k + 1) * P], ident[:, :])
                elif u < TU + WU:
                    if u == TU:
                        pe.wait_ge(s_prepread, count(b, USES, 2 + TU))
                    j = u - TU
                    for k in range(KB):
                        last = pe.matmul(prep_ps[:, u % 2, 0:F + 1], x_cols[:, k, j * P:(j + 1) * P],
                                         w_ext[:, k, :], start=(k == 0), stop=(k == KB - 1))
                else:
                    c = u - TU - WU
                    for k in range(KB):
                        last = pe.matmul(prep_ps[:, u % 2, :], wa1_b[:, k, :],
                                         x_cols[:, k, c * CW:(c + 1) * CW],
                                         start=(k == 0), stop=(k == KB - 1))
                last.then_inc(s_prep, 1)

            def prologue():
                for u in range(USES):
                    prepare((0, 0), u)

            order = [(j, (0, 1)) for j in range(LATE)] + [(j, (2, 3)) for j in range(LATE)] \
                + [(j, range(T)) for j in range(LATE, JB)]

            def steps(b, chunks, prev, more):
                p = b[1] % 2
                for c in chunks:
                    for j, ts in order:
                        n = c * JB + j
                        if n == 0 and 0 in ts:
                            pe.wait_ge(s_prepread, count(b, USES, 2 + USES))
                        if j == 0 and 0 in ts:
                            pe.wait_ge(s_h, count(b, NC * T, 2 * T + T * (c - 2) + T))
                        if j == 0 and 2 in ts:
                            pe.wait_ge(s_h, count(b, NC * T, 2 * T + T * (c - 1) + 2))
                        if 0 in ts:
                            pe.wait_ge(s_e, count(b, STEPS, n + 1))
                        for t in ts:
                            last = pe.matmul(out_ps[:, bank(c, t), 0:F + 1],
                                             e[:, n % ERING, t * P:(t + 1) * P], wh[:, p, j, 1:F + 2],
                                             start=(j == 0), stop=(j == JB - 1))
                        if T - 1 in ts:
                            last.then_inc(s_mm, 1)
                            for u in uses_in(n) if more else ():
                                prepare(following(b), u)

            run(pe, steps, prologue, lambda b: None)

        @block.vector
        def _(dve):
            dve.sem_inc(s_h, 2 * T)
            for s in s_st:
                dve.sem_inc(s, 16)
            dve.wait_ge(s_w, 48)
            for k in range(KB):
                for i, (row, dst) in enumerate(((a1_r, wa1[:, k:k + 1]), (a2_r, w_ext[:, k, 0:1]))):
                    dve.tensor_tensor_reduce(out=trash[:, 2 * k + i, :], in0=w_ext[:, k, 1:F + 1], in1=row[:, :],
                                             scale=1.0, scalar=0.0, op0=ALU.mult, op1=ALU.add,
                                             accum_out=dst).then_inc(s_wa, 1)
            dve.wait_ge(s_wa, 2 * KB)
            dve.wait_ge(s_id, 1)
            for k in range(KB):
                dve.tensor_scalar(wa1_b[:, k, :], a1_r[:, 0:P], 0.0, wa1[:, k:k + 1], ALU.mult, ALU.add)\
                   .then_inc(s_wa, 1)

            def mask_piece(i):
                q, c = divmod(i, NC)
                dve.wait_ge(s_adj[i % 4], 16 * (i // 4 + 1))
                dve.tensor_scalar(mask[:, 4 * q:4 * q + 4, c * CW:(c + 1) * CW],
                                  stages[i % 4].rearrange("p (a i) -> p a i", a=4),
                                  0, -BIG, ALU.is_le, ALU.mult).then_inc(s_mask, 1)

            def fifths(b):
                p = b[1] % 2
                dve.wait_ge(s_prepread, count(b, USES, 2 + TU + WU))
                dve.tensor_scalar(s_fifth[:, p, :], wh[:, p, :, 0], ALPHA, None, ALU.mult)\
                   .then_inc(s_fifths, 1)

            def maximum(b, j):
                p = b[1] % 2
                dve.wait_ge(s_prepread, count(b, USES, 2 + TU + j + 1))
                if j == 0:
                    dve.tensor_scalar(best[:, p, :], mask[:, 0, :], wh[:, p, 0, 0:1], None, ALU.add)\
                       .then_inc(s_best, 1)
                else:
                    dve.wait_ge(s_best, count(b, JB, j))
                    dve.scalar_tensor_tensor(out=best[:, p, :], in0=mask[:, j, :], scalar=wh[:, p, j, 0:1],
                                             in1=best[:, p, :], op0=ALU.add, op1=ALU.max).then_inc(s_best, 1)

            def row_operation(b, k):
                p = b[1] % 2
                if k == 0:
                    dve.wait_ge(s_prepread, count(b, USES, 2 + USES))
                    dve.wait_ge(s_all, count(b, 1, 1))
                    dve.tensor_tensor(low[:, p, :], low[:, p, :], s_row[:, :], ALU.add).then_inc(s_rows, 1)
                if k == 1:
                    dve.wait_ge(s_rows, count(b, 4, 1))
                    dve.scalar_tensor_tensor(out=low[:, p, :], in0=low[:, p, :], scalar=ALPHA, in1=low[:, p, :],
                                             op0=ALU.mult, op1=ALU.max).then_inc(s_rows, 1)
                if k == 2:
                    dve.wait_ge(s_rows, count(b, 4, 2))
                    dve.tensor_tensor(best[:, p, :], s_row[:, :], low[:, p, :], ALU.subtract).then_inc(s_rows, 1)
                if k == 3:
                    dve.scalar_tensor_tensor(out=low[:, p, :], in0=s_row[:, :], scalar=ALPHA, in1=low[:, p, :],
                                             op0=ALU.mult, op1=ALU.subtract).then_inc(s_rows, 1)

            def invert(b, c):
                dve.wait_ge(s_mm, count(b, STEPS, ERING + (c + 1) * JB))
                for t in BANK_ORDER:
                    dve.reciprocal(rden[:, c % 2, t:t + 1], out_ps[:, bank(c, t), F:F + 1]).then_inc(s_rd, 1)

            def elu(b, c):
                dve.wait_ge(s_en, count(b, NC, c + 1))
                dve.scalar_tensor_tensor(out=h[:, c % 2, :, :], in0=h[:, c % 2, :, :], scalar=0.0,
                                         in1=neg[:, :, :], op0=ALU.max, op1=ALU.add).then_inc(s_elu, 1)

            def stats(b, c, t):
                dve.wait_ge(s_r, count(b, NC, c + 1))
                dve.bn_stats(bn[:, t, :], h[:, c % 2, t, :]).then_inc(s_bn, 1)

            def variance(b, c):
                dve.wait_ge(s_bn, count(b, NC * T, T * (c + 1)))
                dve.memset(tick[:, :], 0.0)
                for t in range(T):
                    dve.bn_aggr(mv[:, t, :], bn[:, t, :]).then_inc(s_ag, 1)
                dve.wait_ge(s_ag, count(b, NC * T, T * (c + 1)))
                dve.tensor_scalar(var_eps[:, :], mv[:, :, 1], EPS, None, ALU.add).then_inc(s_ve, 1)

            def offset(b, c):
                dve.wait_ge(s_pw, count(b, NC, c + 1))
                dve.scalar_tensor_tensor(out=nmr[:, :], in0=mv[:, :, 0], scalar=-1.0, in1=rstd[:, :],
                                         op0=ALU.mult, op1=ALU.mult).then_inc(s_rs, 1)

            def prologue():
                for i in range(NC * 4):
                    mask_piece(i)
                    if i % NC == NC - 1 and i >= NC:
                        for j in range(4 * (i // NC - 1), 4 * (i // NC)):
                            dve.wait_ge(s_diag, j + 1)
                            maximum((0, 0), j)
                for j in range(JB - 4, JB):
                    dve.wait_ge(s_diag, j + 1)
                    maximum((0, 0), j)
                fifths((0, 0))
                for k in range(4):
                    row_operation((0, 0), k)
                larger_side((0, 0), 0)

            def larger_side(b, n):
                c, j = divmod(n, JB)
                p = b[1] % 2
                tile = e[:, n % ERING, :]
                if n == 0:
                    dve.wait_ge(s_rows, count(b, 4, 4))
                dve.wait_ge(s_lin, count(b, STEPS, n + 1))
                dve.scalar_tensor_tensor(out=tile, in0=best[:, p, c * CW:(c + 1) * CW],
                                         scalar=wh[:, p, j, 0:1], in1=tile, op0=ALU.add, op1=ALU.max)\
                   .then_inc(s_max, 1)

            def steps(b, chunks, prev, more):
                for c in chunks:
                    before = chunk_before(b, c)
                    for j in range(JB):
                        n = c * JB + j
                        tile = e[:, n % ERING, :]
                        if n + 1 < STEPS:
                            larger_side(b, n + 1)
                        elif more:
                            larger_side(following(b), 0)
                        if j in ON_DVE:
                            dve.wait_ge(s_max, count(b, STEPS, n + 1))
                            dve.tensor_tensor(tile, tile, mask[:, j, c * CW:(c + 1) * CW], ALU.add)\
                               .then_inc(s_log, 1)
                        if prev and j == 2:
                            invert(*before)
                        if prev and j == 6:
                            elu(*before)
                        if prev and j == 10:
                            for t in range(T):
                                stats(*before, t)
                        if prev and j == 11:
                            variance(*before)
                        if prev and j == 13:
                            offset(*before)
                        if more:
                            for m in range(JB):
                                if n == max_at(m):
                                    maximum(following(b), m)
                            if n == max_at(JB - 1) + 1:
                                fifths(following(b))
                            if n in ROWS_AT:
                                row_operation(following(b), ROWS_AT.index(n))

            def tail(b):
                c = NC - 1
                invert(b, c)
                elu(b, c)
                for t in range(T):
                    stats(b, c, t)
                variance(b, c)
                offset(b, c)

            run(dve, steps, prologue, tail)


def build(nc, x, xT, adjT, wqT, wkT, wvT, woT, bq, bk, bv, bo, gamma, beta, W, a, out):
    x1 = nc.dram_tensor("x1", tuple(x.shape), F32, kind="Internal").ap()
    layer0(nc, x, xT, adjT, wqT, wkT, wvT, woT, bq, bk, bv, bo, gamma, beta, x1)
    layer1(nc, x1, adjT, W, a, out)


def kernel(x, adj, L0_gnn_Wq, L0_gnn_bq, L0_gnn_Wk, L0_gnn_bk, L0_gnn_Wv, L0_gnn_bv, L0_gnn_Wo, L0_gnn_bo,
           L0_gnn_gamma, L0_gnn_beta, L1_gnn_W, L1_gnn_a):
    import numpy as np
    import concourse.bacc as bacc
    from concourse.bass_utils import run_bass_kernel_spmd

    x = np.asarray(x)
    arrays = {
        "x": x, "xT": x.transpose(0, 2, 1), "adjT": np.asarray(adj).T,
        "wqT": np.asarray(L0_gnn_Wq).T, "wkT": np.asarray(L0_gnn_Wk).T,
        "wvT": np.asarray(L0_gnn_Wv).T, "woT": np.asarray(L0_gnn_Wo).T,
        "bq": np.asarray(L0_gnn_bq), "bk": np.asarray(L0_gnn_bk), "bv": np.asarray(L0_gnn_bv),
        "bo": np.asarray(L0_gnn_bo), "gamma": np.asarray(L0_gnn_gamma), "beta": np.asarray(L0_gnn_beta),
        "W": np.asarray(L1_gnn_W), "a": np.asarray(L1_gnn_a),
    }
    arrays = {name: np.ascontiguousarray(v) for name, v in arrays.items()}
    nc = bacc.Bacc("TRN2", target_bir_lowering=False, num_devices=1, dynamic_dma_scratch_size=8192)
    args = [nc.dram_tensor(f"in_{name}", v.shape, mybir.dt.from_np(v.dtype), kind="ExternalInput").ap()
            for name, v in arrays.items()]
    out = nc.dram_tensor("out_0", x.shape, F32, kind="ExternalOutput").ap()
    build(nc, *args, out)
    r = run_bass_kernel_spmd(nc, [{f"in_{name}": v for name, v in arrays.items()}], core_ids=[0])
    return r.results[0]["out_0"]
```
